# Optimizing a Trainium2 kernel written in Bass

```python
import numpy as np
import jax
import jax.numpy as jnp

def _softmax(x, axis=-1):
    return jax.nn.softmax(x, axis=axis)

def _gelu(x):
    return jax.nn.gelu(x, approximate=True)

def _silu(x):
    return jax.nn.silu(x)

def _sigmoid(x):
    return jax.nn.sigmoid(x)

def _layernorm(x, axis=-1, eps=1e-05):
    m = jnp.mean(x, axis=axis, keepdims=True)
    v = jnp.var(x, axis=axis, keepdims=True)
    return (x - m) / jnp.sqrt(v + eps)

def _scatter_add(tgt, idx, src, axis=0):
    return tgt.at[idx].add(src)

def _segment_sum(src, seg, n):
    return jax.ops.segment_sum(src, seg, n)
kernel_name = 'mk_xattn_seq_d2_seqx_r4_5fe2f9'

def setup_inputs(seed: int=0):
    np.random.seed(seed)
    _w = jnp.asarray

    def _rec_inputs():
        import jax
        import jax.numpy as jnp
        _rk = jax.random.key(seed)
        x = -0.0005207 + 1.001 * jax.random.normal(jax.random.fold_in(_rk, 1), (32, 256, 256), jnp.float32)
        _lenS = 256 - jax.random.randint(jax.random.fold_in(_rk, 7), (32,), 0, max(1, 256 // 4) + 1, jnp.int32)
        _lenS2 = 120 - jax.random.randint(jax.random.fold_in(_rk, 8), (32,), 0, max(1, 120 // 4) + 1, jnp.int32)
        _ctx_1024P = jax.random.normal(jax.random.fold_in(_rk, 11), (32, 16, 256), jnp.float32)
        _ctx_1024c = jax.random.dirichlet(jax.random.fold_in(_rk, 511), 0.3 * jnp.ones((16,), jnp.float32), (32, 120))
        _ctx_1024t = jnp.einsum('bsk,bkd->bsd', _ctx_1024c, _ctx_1024P)
        _ctx_1024t = _ctx_1024t * jax.lax.rsqrt(jnp.mean(jnp.square(_ctx_1024t)) + 1e-12) * 0.953939
        ctx_1024 = 4.13588e-05 + 0.999923 * (_ctx_1024t + 0.3 * jax.random.normal(jax.random.fold_in(_rk, 611), (32, 120, 256), jnp.float32))
        return (x, ctx_1024)
    x, ctx_1024 = _rec_inputs()

    def _L0_xattn_setup():
        import jax, jax.numpy as jnp
        import numpy as np
        D = 256
        H = 16
        DH = D // H
        FF = 4 * D
        EPS = 1e-05

        def _layer_norm(x, g, b):
            mu = jnp.mean(x, axis=-1, keepdims=True)
            var = jnp.mean(jnp.square(x - mu), axis=-1, keepdims=True)
            return (x - mu) * jax.lax.rsqrt(var + EPS) * g + b
        key = jax.random.key(seed)
        ks = jax.random.split(key, 12)
        B, Lq, Lkv = (2, 256, 1024)
        s = 1.0 / np.sqrt(D)
        sf = 1.0 / np.sqrt(FF)
        return {'Q': jax.random.normal(ks[0], (B, Lq, D), jnp.float32), 'KV': jax.random.normal(ks[1], (B, Lkv, D), jnp.float32), 'Wq': jax.random.normal(ks[2], (D, D), jnp.float32) * s, 'bq': jnp.zeros((D,), jnp.float32), 'Wk': jax.random.normal(ks[3], (D, D), jnp.float32) * s, 'bk': jnp.zeros((D,), jnp.float32), 'Wv': jax.random.normal(ks[4], (D, D), jnp.float32) * s, 'bv': jnp.zeros((D,), jnp.float32), 'Wo': jax.random.normal(ks[5], (D, D), jnp.float32) * s, 'bo': jnp.zeros((D,), jnp.float32), 'W1': jax.random.normal(ks[6], (D, FF), jnp.float32) * s, 'b1': jnp.zeros((FF,), jnp.float32), 'W2': jax.random.normal(ks[7], (FF, D), jnp.float32) * sf, 'b2': jnp.zeros((D,), jnp.float32), 'ln_q_g': jnp.ones((D,), jnp.float32), 'ln_q_b': jnp.zeros((D,), jnp.float32), 'ln_ff_g': jnp.ones((D,), jnp.float32), 'ln_ff_b': jnp.zeros((D,), jnp.float32)}
    _L0_xattn_all = _L0_xattn_setup()
    _L0_xattn_in = {k: v for k, v in _L0_xattn_all.items() if k in ('Wq', 'bq', 'Wk', 'bk', 'Wv', 'bv', 'Wo', 'bo', 'W1', 'b1', 'W2', 'b2', 'ln_q_g', 'ln_q_b', 'ln_ff_g', 'ln_ff_b')}
    del _L0_xattn_all

    def _L1_xattn_setup():
        import jax, jax.numpy as jnp
        import numpy as np
        LN_EPS = 1e-05
        ATTN_EPS = 1e-06
        key = jax.random.key(seed)
        k1, k2, k3 = jax.random.split(key, 3)
        B, Nq, Nk, D = (8, 512, 512, 256)
        return {'query': jax.random.normal(k1, (B, Nq, D), dtype=jnp.float32), 'key': jax.random.normal(k2, (B, Nk, D), dtype=jnp.float32), 'value': jax.random.normal(k3, (B, Nk, D), dtype=jnp.float32), 'gamma': jnp.ones((D,), dtype=jnp.float32), 'beta': jnp.zeros((D,), dtype=jnp.float32)}
    _L1_xattn_all = _L1_xattn_setup()
    _L1_xattn_in = {k: v for k, v in _L1_xattn_all.items() if k in ('gamma', 'beta')}
    del _L1_xattn_all
    return {'x': x, 'ctx_1024': ctx_1024, 'L0_xattn_Wq': _L0_xattn_in['Wq'], 'L0_xattn_bq': _L0_xattn_in['bq'], 'L0_xattn_Wk': _L0_xattn_in['Wk'], 'L0_xattn_bk': _L0_xattn_in['bk'], 'L0_xattn_Wv': _L0_xattn_in['Wv'], 'L0_xattn_bv': _L0_xattn_in['bv'], 'L0_xattn_Wo': _L0_xattn_in['Wo'], 'L0_xattn_bo': _L0_xattn_in['bo'], 'L0_xattn_W1': _L0_xattn_in['W1'], 'L0_xattn_b1': _L0_xattn_in['b1'], 'L0_xattn_W2': _L0_xattn_in['W2'], 'L0_xattn_b2': _L0_xattn_in['b2'], 'L0_xattn_ln_q_g': _L0_xattn_in['ln_q_g'], 'L0_xattn_ln_q_b': _L0_xattn_in['ln_q_b'], 'L0_xattn_ln_ff_g': _L0_xattn_in['ln_ff_g'], 'L0_xattn_ln_ff_b': _L0_xattn_in['ln_ff_b'], 'L1_xattn_gamma': _L1_xattn_in['gamma'], 'L1_xattn_beta': _L1_xattn_in['beta']}

def reference(x, ctx_1024, L0_xattn_Wq, L0_xattn_bq, L0_xattn_Wk, L0_xattn_bk, L0_xattn_Wv, L0_xattn_bv, L0_xattn_Wo, L0_xattn_bo, L0_xattn_W1, L0_xattn_b1, L0_xattn_W2, L0_xattn_b2, L0_xattn_ln_q_g, L0_xattn_ln_q_b, L0_xattn_ln_ff_g, L0_xattn_ln_ff_b, L1_xattn_gamma, L1_xattn_beta):
    import jax
    import jax.numpy as jnp

    def _L0_xattn_ref(Q, KV, Wq, bq, Wk, bk, Wv, bv, Wo, bo, W1, b1, W2, b2, ln_q_g, ln_q_b, ln_ff_g, ln_ff_b):
        import jax, jax.numpy as jnp
        import numpy as np
        D = 256
        H = 16
        DH = D // H
        FF = 4 * D
        EPS = 1e-05

        def _layer_norm(x, g, b):
            mu = jnp.mean(x, axis=-1, keepdims=True)
            var = jnp.mean(jnp.square(x - mu), axis=-1, keepdims=True)
            return (x - mu) * jax.lax.rsqrt(var + EPS) * g + b
        B, Lq, _ = Q.shape
        Lkv = KV.shape[1]
        qn = _layer_norm(Q, ln_q_g, ln_q_b)
        q = (qn @ Wq + bq).reshape(B, Lq, H, DH).transpose(0, 2, 1, 3)
        k = (KV @ Wk + bk).reshape(B, Lkv, H, DH).transpose(0, 2, 1, 3)
        v = (KV @ Wv + bv).reshape(B, Lkv, H, DH).transpose(0, 2, 1, 3)
        scores = jnp.einsum('bhqd,bhkd->bhqk', q, k) / jnp.sqrt(jnp.float32(DH))
        attn = jax.nn.softmax(scores, axis=-1)
        ctx = jnp.einsum('bhqk,bhkd->bhqd', attn, v)
        ctx = ctx.transpose(0, 2, 1, 3).reshape(B, Lq, D)
        x = Q + (ctx @ Wo + bo)
        h = _layer_norm(x, ln_ff_g, ln_ff_b)
        ff = jax.nn.silu(h @ W1 + b1) @ W2 + b2
        return x + ff

    def _L1_xattn_ref(query, key, value, gamma, beta):
        import jax, jax.numpy as jnp
        import numpy as np
        LN_EPS = 1e-05
        ATTN_EPS = 1e-06
        Q_phi = jax.nn.elu(query)
        K_phi = jax.nn.elu(key)
        KV = jnp.einsum('bnd,bne->bde', K_phi, value)
        Z = 1.0 / (jnp.einsum('bnd,bd->bn', Q_phi, K_phi.sum(axis=1)) + ATTN_EPS)
        attn = jnp.einsum('bnd,bde->bne', Q_phi, KV) * Z[..., None]
        x = query + attn
        mean = jnp.mean(x, axis=-1, keepdims=True)
        var = jnp.mean(jnp.square(x - mean), axis=-1, keepdims=True)
        return (x - mean) * jax.lax.rsqrt(var + LN_EPS) * gamma + beta
    x = _L0_xattn_ref(x, ctx_1024, L0_xattn_Wq, L0_xattn_bq, L0_xattn_Wk, L0_xattn_bk, L0_xattn_Wv, L0_xattn_bv, L0_xattn_Wo, L0_xattn_bo, L0_xattn_W1, L0_xattn_b1, L0_xattn_W2, L0_xattn_b2, L0_xattn_ln_q_g, L0_xattn_ln_q_b, L0_xattn_ln_ff_g, L0_xattn_ln_ff_b)
    x = _L1_xattn_ref(x, ctx_1024, ctx_1024, L1_xattn_gamma, L1_xattn_beta)
    return x

_drawn_inputs = setup_inputs


def setup_inputs(seed=0):
    import zlib

    import numpy as np

    out = dict(_drawn_inputs(seed))
    spreads = {'L0_xattn_bq': (0.0, 0.1),
     'L0_xattn_bk': (0.0, 0.1),
     'L0_xattn_bv': (0.0, 0.1),
     'L0_xattn_bo': (0.0, 0.1),
     'L0_xattn_b1': (0.0, 0.1),
     'L0_xattn_b2': (0.0, 0.1),
     'L0_xattn_ln_q_g': (1.0, 0.2),
     'L0_xattn_ln_q_b': (0.0, 0.1),
     'L0_xattn_ln_ff_g': (1.0, 0.2),
     'L0_xattn_ln_ff_b': (0.0, 0.1),
     'L1_xattn_gamma': (1.0, 0.2),
     'L1_xattn_beta': (0.0, 0.1)}
    factors = {}
    for name, (base, spread) in spreads.items():
        noise = np.random.default_rng([zlib.crc32(name.encode()), seed]).standard_normal(out[name].shape)
        drawn = base * np.exp(spread * noise) if base else spread * noise
        out[name] = jnp.asarray(drawn.astype(out[name].dtype))
    for name, factor in factors.items():
        out[name] = (out[name] * factor).astype(out[name].dtype)
    return out
```

```python
from collections import namedtuple
from contextlib import ExitStack

import concourse.bass as bass
from concourse import mybir

F32 = mybir.dt.float32
F32R = mybir.dt.float32r
ALU = mybir.AluOpType
ACT = mybir.ActivationFunctionType
AX = mybir.AxisListType

Batch = namedtuple("Batch", "half slot")


def number(b):
    return 2 * b.half + b.slot


def following(b):
    return Batch(b.half, 1) if b.slot == 0 else Batch(b.half + 1, 0)


def preceding(b):
    return Batch(b.half, 0) if b.slot == 1 else Batch(b.half - 1, 1)


def done(b, per=1, k=None):
    return per * number(b) + (per if k is None else k)


def wait(eng, sem, count):
    if not isinstance(count, int) or count > 0:
        eng.wait_ge(sem, count)


def build(nc, x, ctx, Wq, bq, Wk, bk, Wv, bv, Wo, bo, W1, b1, W2, b2,
          ln_q_g, ln_q_b, ln_ff_g, ln_ff_b, gamma, beta, out):
    P = 128
    B, LQ, D = x.shape
    LK = ctx.shape[1]
    FF = W1.shape[1]
    H = 16
    DH = D // H
    QT = LQ // P
    KD = D // P
    PAIRS = H // 2
    NU = FF // (2 * P)
    BANK = 512
    VW = 32
    KVW = D + 2
    PARTS = 3
    LN_EPS = 1e-5
    Z_EPS = 1e-6
    SCALE = float(DH) ** -0.5
    assert QT == 2 and KD == 2 and B % 2 == 0 and B >= 4 and QT * D == BANK and SCALE == 0.25

    es = ExitStack()
    with es:
        def sb(name, shape, dt=F32):
            return es.enter_context(nc.sbuf_tensor(name, shape, dt))

        def sem(name):
            return es.enter_context(nc.semaphore(name))

        wq_hi, wq_lo = sb("wq_hi", [P, KD, D], F32R), sb("wq_lo", [P, KD, D], F32R)
        wk_hi, wk_lo = sb("wk_hi", [P, KD, D], F32R), sb("wk_lo", [P, KD, D], F32R)
        wv_hi, wv_lo = sb("wv_hi", [P, KD, D], F32R), sb("wv_lo", [P, KD, D], F32R)
        wo_hi, wo_lo = sb("wo_hi", [P, KD, D], F32R), sb("wo_lo", [P, KD, D], F32R)
        w1_hi, w1_lo = sb("w1_hi", [P, KD, FF], F32R), sb("w1_lo", [P, KD, FF], F32R)
        w2_hi, w2_lo = sb("w2_hi", [P, FF // P, D], F32R), sb("w2_lo", [P, FF // P, D], F32R)
        cols = sb("cols", [P, 7, KD])
        bq_sum, bq_col = sb("bq_sum", [P, KD]), sb("bq_col", [P, KD])
        b1_stat = sb("b1_stat", [P, FF], F32R)
        ones = sb("ones", [P, LQ])
        ones_r = sb("ones_r", [P, LQ], F32R)
        bv_wide = sb("bv_wide", [P, KD, P])
        bo_all, b2_all = sb("bo_all", [P, D]), sb("b2_all", [P, D])
        gamma_all, beta_all = sb("gamma_all", [P, D]), sb("beta_all", [P, D])
        ident = sb("ident", [P, P])
        minus_half = sb("minus_half", [P, QT])

        xs = sb("xs", [P, 2, QT, D])
        cs = sb("cs", [LK, 2, D])
        x_bo = sb("x_bo", [P, 2, QT, D])
        stats = sb("stats", [P, 3, QT, 6])
        mv = sb("mv", [P, 3, QT, 2])
        var_eps = sb("var_eps", [P, 3, QT])
        rstd = sb("rstd", [P, 3, QT])
        xn = sb("xn", [P, QT, D])
        xT_hi, xT_lo = sb("xT_hi", [P, KD, LQ], F32R), sb("xT_lo", [P, KD, LQ], F32R)
        cT_hi, cT_lo = sb("cT_hi", [P, KD, LK], F32R), sb("cT_lo", [P, KD, LK], F32R)
        q_hi, q_lo = sb("q_hi", [P, KD, LQ], F32R), sb("q_lo", [P, KD, LQ], F32R)
        k_hi, k_lo = sb("k_hi", [P, KD, LK], F32R), sb("k_lo", [P, KD, LK], F32R)
        q_stack = sb("q_stack", [P, PAIRS, LQ], F32R)
        k_stack = sb("k_stack", [P, PAIRS, 2, LK], F32R)
        v_aug = sb("v_aug", [LK, H, VW])
        neg_max = sb("neg_max", [P, QT, H])
        max_parts = sb("max_parts", [P, QT, 4 * PAIRS], F32R)
        max_T = sb("max_T", [4 * PAIRS, LQ], F32R)
        probs = sb("probs", [LK, H, LQ])
        aug = sb("aug", [P, H // 4, LQ])
        den_inv = sb("den_inv", [P, QT, H])
        cn = sb("cn", [P, QT, D])
        cnT_hi, cnT_lo = sb("cnT_hi", [P, KD, LQ], F32R), sb("cnT_lo", [P, KD, LQ], F32R)
        c_min, c_exp, k_phi = sb("c_min", [LK, D]), sb("c_exp", [LK, D]), sb("k_phi", [LK, D])
        c_hi, c_lo = sb("c_hi", [LK, KVW], F32R), sb("c_lo", [LK, KVW], F32R)
        kp_hi, kp_lo = sb("kp_hi", [LK, D], F32R), sb("kp_lo", [LK, D], F32R)
        kv_hi, kv_lo = sb("kv_hi", [P, 2, KD, KVW], F32R), sb("kv_lo", [P, 2, KD, KVW], F32R)
        x1, x1_b2, hn = sb("x1", [P, QT, D]), sb("x1_b2", [P, QT, D]), sb("hn", [P, QT, D])
        hT_hi, hT_lo = sb("hT_hi", [P, KD, LQ], F32R), sb("hT_lo", [P, KD, LQ], F32R)
        th = sb("th", [P, 2, BANK])
        act_f = sb("act_f", [P, NU, BANK])
        a_hi, a_lo = sb("a_hi", [P, NU, BANK], F32R), sb("a_lo", [P, NU, BANK], F32R)
        x2_tiles = sb("x2_tiles", [P, 4, QT, D])
        x2, x2_min, x2_exp, q_phi = (x2_tiles[:, i] for i in range(4))
        qpT_hi, qpT_lo = sb("qpT_hi", [P, KD, LQ], F32R), sb("qpT_lo", [P, KD, LQ], F32R)
        z_den, z_inv = sb("z_den", [P, QT]), sb("z_inv", [P, QT])
        x3_tiles = sb("x3_tiles", [P, 4, QT, D])
        x3, y, yg, y_out = (x3_tiles[:, i] for i in range(4))
        mean_shift = sb("mean_shift", [P, QT])

        rows = probs[0:1].rearrange("o h q -> o (h q)")[:, 0:4 * D + FF]
        b1_row = th[0:1].rearrange("o i n -> o (i n)")
        w1_in = act_f[:].rearrange("p u (i n) -> p (u i n)", i=2).rearrange("p (k n) -> p k n", k=KD)
        w2_in = x2_tiles[:].rearrange("p i t e -> p (i t e)").rearrange("p (c n) -> p c n", n=D)
        wqkvo_in = x3_tiles[:].rearrange("p i t e -> p (i t e)").rearrange("p (i k n) -> p i k n", i=4, k=KD)

        S = es.enter_context(nc.psum_tensor("S", [P, 4, BANK], F32))
        X = es.enter_context(nc.psum_tensor("X", [P, 4, BANK], F32))

        w_loaded, small_loaded = sem("w_loaded"), sem("small_loaded")
        passed, dve_consts, dve_setup, pe_setup, stacks_set, ident_set = (
            sem(n) for n in ("passed", "dve_consts", "dve_setup", "pe_setup", "stacks_set", "ident_set"))
        x_loaded = [sem(f"x_loaded{i}") for i in range(2)]
        c_loaded = [sem(f"c_loaded{i}") for i in range(2)]
        q_stacked, k_stacked, max_stacked, stored = (sem(n) for n in ("q_stacked", "k_stacked", "max_stacked", "stored"))
        xT_ps, cT_ps, q_ps, k_ps, v_ps, kv_ps, s_ps, maxT_ps, st_ps, pv_ps, aug_ps = (
            sem(n) for n in ("xT_ps", "cT_ps", "q_ps", "k_ps", "v_ps", "kv_ps", "s_ps", "maxT_ps", "st_ps", "pv_ps", "aug_ps"))
        cnT_ps, wo_ps, hT_ps, f1_ps, f2_ps, qpT_ps, la_ps = (
            sem(n) for n in ("cnT_ps", "wo_ps", "hT_ps", "f1_ps", "f2_ps", "qpT_ps", "la_ps"))
        xT_hid, cT_hid, q_hid, k_hid, v_copied, c_exped, kv_hid, probs_set, aug_set = (
            sem(n) for n in ("xT_hid", "cT_hid", "q_hid", "k_hid", "v_copied", "c_exped", "kv_hid", "probs_set", "aug_set"))
        cnT_hid, hT_hid, th_set, a_hid, x2_exped, qpT_hid = (
            sem(n) for n in ("cnT_hid", "hT_hid", "th_set", "a_hid", "x2_exped", "qpT_hid"))
        stat1, mv1, xn_set, xT_split, cT_split, q_split, k_split, k_phi_set, kp_hid, kp_split, kv_split = (
            sem(n) for n in ("stat1", "mv1", "xn_set", "xT_split", "cT_split", "q_split", "k_split", "k_phi_set", "kp_hid",
                             "kp_split", "kv_split"))
        max_set, max_hid, max_split, maxT_set, den_set, cn_set, cnT_split = (
            sem(n) for n in ("max_set", "max_hid", "max_split", "maxT_set", "den_set", "cn_set", "cnT_split"))
        x1_set, stat2, mv2, hn_set, hT_split, act_set, x2_set, q_phi_set, qpT_split, z_set, z_inved, x3_set, stat3, mv3 = (
            sem(n) for n in ("x1_set", "stat2", "mv2", "hn_set", "hT_split", "act_set", "x2_set", "q_phi_set", "qpT_split",
                             "z_set", "z_inved", "x3_set", "stat3", "mv3"))
        c_mined, c_hid, c_split, x_bo_set, var1, rstd1, var2, rstd2, x1_b2_set, a_split, x2_mined, var3, rstd3 = (
            sem(n) for n in ("c_mined", "c_hid", "c_split", "x_bo_set", "var1", "rstd1", "var2", "rstd2", "x1_b2_set",
                             "a_split", "x2_mined", "var3", "rstd3"))
        shift_set, y_set, yg_set, y_out_set = (sem(n) for n in ("shift_set", "y_set", "yg_set", "y_out_set"))

        W_COUNT, SMALL_COUNT, SETUP_STEPS = 16 * 6, 16 * 12, 7

        block = es.enter_context(nc.Block())

        def periods(eng, period):
            period(eng, Batch(0, 0), None)
            period(eng, Batch(0, 1), Batch(0, 0))
            with eng.Fori(1, B // 2 - 1) as j:
                period(eng, Batch(j, 0), Batch(j - 1, 1))
                period(eng, Batch(j, 1), Batch(j, 0))
            last = Batch(B // 2 - 1, 1)
            period(eng, preceding(last), preceding(preceding(last)))
            period(eng, last, preceding(last))
            period(eng, None, last)

        def settled(eng):
            eng.sem_inc(passed)

        def is_first(b):
            return isinstance(b.half, int) and b == Batch(0, 0)

        def is_last(b):
            return isinstance(b.half, int) and b == Batch(B // 2 - 1, 1)

        @block.sync
        def _(sp):
            def load(b):
                for sem_ in (xn_set, x_bo_set, cT_ps, k_phi_set, c_split):
                    wait(sp, sem_, number(b) - 1)
                sp.dma_start(xs[:, b.slot], x[bass.ds(number(b), 1)].rearrange("b (t p) d -> p (b t) d", p=P)
                             ).then_inc(x_loaded[b.slot], 16)
                sp.dma_start(cs[:, b.slot], ctx[bass.ds(number(b), 1)].rearrange("b k d -> k (b d)")
                             ).then_inc(c_loaded[b.slot], 16)

            load(Batch(0, 0))
            for i, v in enumerate((bq, bk, bv, ln_q_g, ln_q_b, ln_ff_g, ln_ff_b)):
                sp.dma_start(cols[:, i], v.rearrange("(k p) -> p k", p=P), allow_slow_non_contiguous=True).then_inc(small_loaded, 16)
            for i, v in enumerate((bo, b2, gamma, beta)):
                sp.dma_start(rows[:, i * D:(i + 1) * D], v.rearrange("(a d) -> a d", a=1)).then_inc(small_loaded, 16)
            sp.dma_start(rows[:, 4 * D:], b1.rearrange("(a d) -> a d", a=1)).then_inc(small_loaded, 16)
            for i, w in enumerate((Wq, Wk, Wv, Wo)):
                sp.dma_start(wqkvo_in[:, i], w.rearrange("(k p) n -> p k n", p=P)).then_inc(w_loaded, 16)
            sp.dma_start(w1_in, W1.rearrange("(k p) n -> p k n", p=P)).then_inc(w_loaded, 16)
            sp.dma_start(w2_in, W2.rearrange("(k p) n -> p k n", p=P)).then_inc(w_loaded, 16)

            def store(d):
                sp.wait_ge(y_out_set, done(d))
                sp.dma_start(out[bass.ds(number(d), 1)].rearrange("b (t p) d -> p (b t) d", p=P), y_out
                             ).then_inc(stored, 16)

            def period(sp, a, d):
                if a is not None:
                    if not is_last(a):
                        load(following(a))
                    if is_first(a):
                        sp.wait_ge(stacks_set, 6)
                    wait(sp, st_ps, PAIRS * number(a))
                    settled(sp)
                    sp.wait_ge(k_split, done(a))
                    settled(sp)
                    for part, src in enumerate((k_hi, k_lo, k_hi)):
                        for ab in range(2):
                            for j in range(P // 32):
                                r, s = 32 * part + DH * ab, 32 * j + DH * ab
                                sp.dma_start(
                                    k_stack[r:r + DH].rearrange("d (g j) a k -> d j a g k", g=KD)[:, j, ab].bitcast(F32),
                                    src[s:s + DH].bitcast(F32)).then_inc(k_stacked, 16)
                    sp.wait_ge(q_split, done(a))
                    for part, src in enumerate((q_hi, q_hi, q_lo)):
                        for j in range(P // 32):
                            sp.dma_start(
                                q_stack[32 * part:32 * part + 32].rearrange("r (g j) q -> r j g q", g=KD)[:, j].bitcast(F32),
                                src[32 * j:32 * j + 32].bitcast(F32)).then_inc(q_stacked, 16)
                if d is not None and not is_first(d):
                    store(preceding(d))
                if a is not None:
                    sp.wait_ge(maxT_set, done(a))
                    sp.dma_start(q_stack[96:100].bitcast(F32), max_T[:].bitcast(F32)).then_inc(max_stacked, 16)

            periods(sp, period)
            store(Batch(B // 2 - 1, 1))
            sp.wait_ge(stored, 16 * B)

        K_DMAS, Q_DMAS = PARTS * 2 * (P // 32), PARTS * (P // 32)

        @block.tensor
        def _(pe):
            def split_mm(out_, stat, mov, n):
                parts = [(c, s, m) for c in range(n) for s, m in ((0, 1), (1, 0), (0, 0))]
                for i, (c, s, m) in enumerate(parts):
                    last = nc.tensor.matmul(out_, stat(c, s), mov(c, m), start=(i == 0), stop=(i == len(parts) - 1))
                return last

            pe.wait_ge(w_loaded, W_COUNT)
            pe.wait_ge(small_loaded, SMALL_COUNT)
            for m in range(KD):
                for k in range(KD):
                    last = nc.tensor.matmul(X[:, 0, m:m + 1], wqkvo_in[:, 0, k, m * P:(m + 1) * P], cols[:, 4, k:k + 1],
                                            start=(k == 0), stop=(k == KD - 1))
            last.then_inc(pe_setup, 1)
            for n in range(FF // BANK):
                for k in range(KD):
                    last = nc.tensor.matmul(S[0:1, n, :], cols[:, 6, k:k + 1], w1_in[:, k, n * BANK:(n + 1) * BANK],
                                            start=(k == 0), stop=(k == KD - 1))
            last.then_inc(pe_setup, 1)
            pe.wait_ge(dve_consts, 2)
            for k in range(KD):
                nc.tensor.matmul(X[:, 1, 0:D], bv_wide[:, k], wqkvo_in[:, 3, k], start=(k == 0), stop=False)
            nc.tensor.matmul(X[:, 1, 0:D], ones[0:1, 0:P], rows[:, 0:D], start=False, stop=True).then_inc(pe_setup, 1)
            for i in range(1, 4):
                bank = (X[:, 2, 0:D], X[:, 2, D:2 * D], X[:, 3, 0:D])[i - 1]
                last = nc.tensor.matmul(bank, ones[0:1, 0:P], rows[:, i * D:(i + 1) * D], start=True, stop=True)
            last.then_inc(pe_setup, 1)
            pe.wait_ge(ident_set, 2)
            pe.wait_ge(dve_setup, SETUP_STEPS)
            pe.wait_ge(stacks_set, 6)

            def context_rows(a):
                pe.wait_ge(c_loaded[a.slot], 16 * (a.half + 1))
                wait(pe, aug_set, 2 * number(a))
                for k in range(KD):
                    last = nc.tensor.transpose(X[:, 2, k * LK:(k + 1) * LK], cs[:, a.slot, k * P:(k + 1) * P],
                                               ident[0:LK, 0:LK])
                last.then_inc(cT_ps, 1)

            def x_rows(a):
                pe.wait_ge(xn_set, done(a))
                wait(pe, qpT_split, number(a) - 1)
                for k in range(KD):
                    for t in range(QT):
                        last = nc.tensor.transpose(X[:, 1, k * LQ + t * P:k * LQ + (t + 1) * P],
                                                   xn[:, t, k * P:(k + 1) * P], ident[:])
                last.then_inc(xT_ps, 1)

            def project_q(a, d):
                pe.wait_ge(xT_split, done(a))
                if d is not None:
                    pe.wait_ge(cnT_split, done(d))
                for g in range(KD):
                    last = split_mm(X[:, 0, g * LQ:(g + 1) * LQ],
                                    lambda c, s: (wq_hi, wq_lo)[s][:, c, g * P:(g + 1) * P],
                                    lambda c, m: (xT_hi, xT_lo)[m][:, c], KD)
                last.then_inc(q_ps, 1)

            def project_k(a):
                pe.wait_ge(cT_split, done(a))
                for g in range(KD):
                    last = split_mm(X[:, 1, g * LK:(g + 1) * LK],
                                    lambda c, s: (wk_hi, wk_lo)[s][:, c, g * P:(g + 1) * P],
                                    lambda c, m: (cT_hi, cT_lo)[m][:, c], KD)
                last.then_inc(k_ps, 1)

            def project_v(a):
                split_mm(X[0:LK, 2, 0:D], lambda c, s: (cT_hi, cT_lo)[s][:, c],
                         lambda c, m: (wv_hi, wv_lo)[m][:, c], KD).then_inc(v_ps, 1)

            def linear_state(a):
                pe.wait_ge(kp_split, done(a))
                pe.wait_ge(c_split, done(a))
                pe.wait_ge(q_split, done(a))
                pe.wait_ge(k_split, done(a))
                for c in range(KD):
                    split_mm(X[:, c, 0:KVW], lambda _, s: (kp_hi, kp_lo)[s][:, c * P:(c + 1) * P],
                             lambda _, m: (c_hi, c_lo)[m][:], 1).then_inc(kv_ps, 1)

            def scores(a, t):
                if t == 0:
                    pe.wait_ge(k_stacked, 16 * K_DMAS * done(a))
                    pe.wait_ge(q_stacked, 16 * Q_DMAS * done(a))
                    wait(pe, cn_set, number(a))
                    wait(pe, x3_set, number(a) - 1)
                else:
                    pe.wait_ge(max_set, done(a, QT, t))
                for p in range(PAIRS):
                    last = nc.tensor.matmul(S[:, p // 2, (p % 2) * 2 * LK:(p % 2 + 1) * 2 * LK],
                                            q_stack[0:96, p, t * P:(t + 1) * P],
                                            k_stack[0:96, p].rearrange("r a k -> r (a k)"), start=True, stop=True)
                last.then_inc(s_ps, 1)

            def max_rows(a):
                pe.wait_ge(max_split, done(a))
                pe.wait_ge(kv_split, done(a, KD))
                for t in range(QT):
                    last = nc.tensor.transpose(X[0:4 * PAIRS, 1, t * P:(t + 1) * P], max_parts[:, t].bitcast(F32), ident[:])
                last.then_inc(maxT_ps, 1)

            def scores_T(a, p):
                if p == 0:
                    pe.wait_ge(max_stacked, 16 * done(a))
                    pe.wait_ge(max_set, done(a, QT))
                if p >= 4:
                    pe.wait_ge(probs_set, done(a, PAIRS, p - 3))
                for ab in range(2):
                    last = nc.tensor.matmul(S[0:LK, p % 4, ab * LQ:(ab + 1) * LQ], k_stack[0:100, p, ab],
                                            q_stack[0:100, p], start=True, stop=True)
                last.then_inc(st_ps, 1)

            def attend(a, G):
                pe.wait_ge(probs_set, done(a, PAIRS, 2 * G + 2))
                if G == 0:
                    pe.wait_ge(v_copied, done(a))
                for c in range(4):
                    h = 4 * G + c
                    last = nc.tensor.matmul(X[32 * c:32 * c + VW, 2 + G // 2, (G % 2) * LQ:(G % 2 + 1) * LQ],
                                            v_aug[:, h], probs[:, h], start=True, stop=True)
                if G % 2 == 1:
                    last.then_inc(pv_ps, 1)

            def attention_rows(a):
                pe.wait_ge(aug_set, done(a, 2))
                pe.wait_ge(probs_set, done(a, PAIRS))
                for t in range(QT):
                    for G in range(H // 4):
                        last = nc.tensor.transpose(S[:, t, G * P:(G + 1) * P], aug[:, G, t * P:(t + 1) * P], ident[:])
                last.then_inc(aug_ps, 1)

            def rows_to_columns(bank, src):
                for k in range(KD):
                    for t in range(QT):
                        last = nc.tensor.transpose(X[:, bank, k * LQ + t * P:k * LQ + (t + 1) * P],
                                                   src[:, t, k * P:(k + 1) * P], ident[:])
                return last

            def project_o(d):
                pe.wait_ge(cnT_split, done(d))
                pe.wait_ge(aug_set, done(d, 2))
                for t in range(QT):
                    last = split_mm(X[:, 3, t * D:(t + 1) * D], lambda c, s: (cnT_hi, cnT_lo)[s][:, c, t * P:(t + 1) * P],
                                    lambda c, m: (wo_hi, wo_lo)[m][:, c], KD)
                last.then_inc(wo_ps, 1)

            def ffn_up(d, a, u):
                if u == 0:
                    pe.wait_ge(hT_split, done(d))
                    if a is not None:
                        pe.wait_ge(v_copied, done(a))
                if u >= 2:
                    pe.wait_ge(act_set, done(d, NU, u - 1))
                for i in range(2):
                    m = 2 * u + i
                    o = X[:, 2 + u % 2, i * LQ:(i + 1) * LQ]
                    nc.tensor.matmul(o, b1_stat[:, m * P:(m + 1) * P], ones_r[:], start=True, stop=False)
                    parts = [(c, s, v) for c in range(KD) for s, v in ((0, 1), (1, 0), (0, 0))]
                    for n, (c, s, v) in enumerate(parts):
                        last = nc.tensor.matmul(o, (w1_hi, w1_lo)[s][:, c, m * P:(m + 1) * P], (hT_hi, hT_lo)[v][:, c],
                                                start=False, stop=(n == len(parts) - 1))
                last.then_inc(f1_ps, 1)

            def ffn_down(d, a, t):
                if t == 0 and a is not None:
                    pe.wait_ge(kv_split, done(a, KD, 1))
                n = 0
                for u in range(NU):
                    if t == 0:
                        pe.wait_ge(a_split, done(d, NU, u + 1))
                    for i in range(2):
                        for s, v in ((0, 1), (1, 0), (0, 0)):
                            lo = i * LQ + t * P
                            last = nc.tensor.matmul(X[:, 0, t * D:(t + 1) * D], (a_hi, a_lo)[s][:, u, lo:lo + P],
                                                    (w2_hi, w2_lo)[v][:, 2 * u + i], start=(n == 0),
                                                    stop=(n == NU * 2 * PARTS - 1))
                            n += 1
                if t == QT - 1:
                    last.then_inc(f2_ps, 1)

            def linear_attention(d, a):
                pe.wait_ge(qpT_split, done(d))
                pe.wait_ge(kv_split, done(d, KD))
                if a is not None:
                    pe.wait_ge(probs_set, done(a, PAIRS))
                for t in range(QT):
                    split_mm(S[:, 2 + t, 0:KVW], lambda c, s: (qpT_hi, qpT_lo)[s][:, c, t * P:(t + 1) * P],
                             lambda c, m: (kv_hi, kv_lo)[m][:, d.slot, c], KD).then_inc(la_ps, 1)

            def period(pe, a, d):
                if d is not None:
                    pe.wait_ge(cn_set, done(d))
                    wait(pe, x2_set, number(d))
                    rows_to_columns(0, cn).then_inc(cnT_ps, 1)
                if a is not None:
                    x_rows(a)
                    context_rows(a)
                if d is not None:
                    project_o(d)
                if a is not None:
                    project_q(a, d)
                    project_k(a)
                    project_v(a)
                if d is not None:
                    pe.wait_ge(hn_set, done(d))
                    rows_to_columns(3, hn).then_inc(hT_ps, 1)
                if a is not None:
                    linear_state(a)
                if d is not None:
                    ffn_up(d, a, 0)
                    ffn_up(d, a, 1)
                if a is not None:
                    scores(a, 0)
                if d is not None:
                    ffn_up(d, a, 2)
                    ffn_up(d, a, 3)
                if a is not None:
                    scores(a, 1)
                if d is not None:
                    ffn_down(d, a, 0)
                if a is not None:
                    max_rows(a)
                if d is not None:
                    ffn_down(d, a, 1)
                if a is not None:
                    for p in range(4):
                        scores_T(a, p)
                    if d is not None:
                        pe.wait_ge(act_set, done(d, NU))
                    attend(a, 0)
                    scores_T(a, 4)
                    scores_T(a, 5)
                    attend(a, 1)
                    scores_T(a, 6)
                    scores_T(a, 7)
                if d is not None:
                    pe.wait_ge(q_phi_set, done(d))
                    if a is not None:
                        pe.wait_ge(maxT_set, done(a))
                    rows_to_columns(1, q_phi).then_inc(qpT_ps, 1)
                if a is not None:
                    attend(a, 2)
                    attend(a, 3)
                    attention_rows(a)
                if d is not None:
                    linear_attention(d, a)

            periods(pe, period)

        @block.scalar
        def _(act):
            def period(act, a, d):
                if d is not None:
                    act.wait_ge(cnT_ps, done(d))
                    wait(act, wo_ps, number(d))
                    nc.scalar.copy(cnT_hi[:], X[:, 0].rearrange("p (k q) -> p k q", k=KD)).then_inc(cnT_hid, 1)
                if a is not None:
                    act.wait_ge(xT_ps, done(a))
                    wait(act, q_ps, number(a))
                    nc.scalar.copy(xT_hi[:], X[:, 1].rearrange("p (k q) -> p k q", k=KD)).then_inc(xT_hid, 1)
                    act.wait_ge(cT_ps, done(a))
                    wait(act, v_ps, number(a))
                    nc.scalar.copy(cT_hi[:], X[:, 2, 0:KD * LK].rearrange("p (k q) -> p k q", k=KD)).then_inc(cT_hid, 1)
                    act.wait_ge(c_mined, done(a))
                    wait(act, k_phi_set, number(a))
                    nc.scalar.activation(c_exp[:], c_min[:], ACT.Exp).then_inc(c_exped, 1)
                    act.wait_ge(q_ps, done(a))
                    wait(act, q_stacked, 16 * Q_DMAS * number(a))
                    for g in range(KD):
                        nc.scalar.activation(q_hi[:, g], X[:, 0, g * LQ:(g + 1) * LQ], ACT.Identity,
                                             bias=bq_col[:, g:g + 1]).then_inc(q_hid, 1)
                    act.wait_ge(k_ps, done(a))
                    wait(act, k_stacked, 16 * K_DMAS * number(a))
                    for g in range(KD):
                        nc.scalar.activation(k_hi[:, g], X[:, 1, g * LK:(g + 1) * LK], ACT.Identity,
                                             bias=cols[:, 1, g:g + 1]).then_inc(k_hid, 1)
                    act.wait_ge(v_ps, done(a))
                    wait(act, pv_ps, 2 * number(a))
                    nc.scalar.copy(v_aug[:, :, 0:DH], X[0:LK, 2, 0:D].rearrange("k (h e) -> k h e", h=H)).then_inc(v_copied, 1)
                if d is not None:
                    act.wait_ge(hT_ps, done(d))
                    wait(act, f1_ps, NU * number(d))
                    nc.scalar.copy(hT_hi[:], X[:, 3].rearrange("p (k q) -> p k q", k=KD)).then_inc(hT_hid, 1)
                if a is not None:
                    wait(act, la_ps, QT * (number(a) - 1))
                    for c in range(KD):
                        act.wait_ge(kv_ps, done(a, KD, c + 1))
                        nc.scalar.copy(kv_hi[:, a.slot, c], X[:, c, 0:KVW]).then_inc(kv_hid, 1)
                if d is not None:
                    def hidden_hi(u):
                        act.wait_ge(act_set, done(d, NU, u + 1))
                        if u == 0:
                            wait(act, f2_ps, number(d))
                        nc.scalar.copy(a_hi[:, u], act_f[:, u]).then_inc(a_hid, 1)

                    for u in range(NU):
                        act.wait_ge(f1_ps, done(d, NU, u + 1))
                        wait(act, act_set, done(d, NU, u - 1))
                        nc.scalar.activation(th[:, u % 2], X[:, 2 + u % 2], ACT.Tanh, scale=0.5).then_inc(th_set, 1)
                        if u > 0:
                            hidden_hi(u - 1)
                    hidden_hi(NU - 1)

                def exponentiate(p):
                    act.wait_ge(st_ps, done(a, PAIRS, p + 1))
                    nc.scalar.activation(probs[:, 2 * p:2 * p + 2], S[0:LK, p % 4].rearrange("k (h q) -> k h q", h=2),
                                         ACT.Exp).then_inc(probs_set, 1)

                if a is not None:
                    wait(act, pv_ps, 2 * number(a))
                    for p in range(4):
                        exponentiate(p)
                if d is not None:
                    act.wait_ge(x2_mined, done(d))
                    nc.scalar.activation(x2_exp, x2_min, ACT.Exp).then_inc(x2_exped, 1)
                if a is not None:
                    for p in range(4, PAIRS):
                        exponentiate(p)
                if d is not None:
                    act.wait_ge(qpT_ps, done(d))
                    wait(act, la_ps, QT * number(d))
                    nc.scalar.copy(qpT_hi[:], X[:, 1].rearrange("p (k q) -> p k q", k=KD)).then_inc(qpT_hid, 1)
                if a is not None:
                    wait(act, aug_ps, number(a))
                    for i in range(2):
                        act.wait_ge(pv_ps, done(a, 2, i + 1))
                        nc.scalar.copy(aug[:, 2 * i:2 * i + 2], X[:, 2 + i].rearrange("p (g q) -> p g q", g=2)
                                       ).then_inc(aug_set, 1)

            act.wait_ge(dve_setup, SETUP_STEPS)
            act.wait_ge(stacks_set, 6)
            act.wait_ge(small_loaded, SMALL_COUNT)
            periods(act, period)

        @block.vector
        def _(dve):
            V = nc.vector
            V.memset(ones[:], 1.0).then_inc(dve_consts, 1)
            dve.wait_ge(dve_consts, 1)
            dve.wait_ge(small_loaded, SMALL_COUNT)
            for k in range(KD):
                last = V.tensor_scalar(bv_wide[:, k], ones[:, 0:P], cols[:, 2, k:k + 1], None, ALU.mult)
            last.then_inc(dve_consts, 1)
            V.memset(minus_half[:], -0.5).then_inc(dve_consts, 1)
            V.memset(k_stack[:].bitcast(F32), 0.0).then_inc(stacks_set, 1)
            V.memset(v_aug[:], 0.0).then_inc(stacks_set, 1)
            V.tensor_copy(ones_r[:], ones[:])
            dve.wait_ge(stacks_set, 2)
            V.memset(v_aug[:, :, DH:DH + 1], 1.0).then_inc(stacks_set, 1)
            V.memset(k_stack[96:98, :, 0, :].bitcast(F32), 1.0).then_inc(stacks_set, 1)
            V.memset(k_stack[96:100, :, 1, :].bitcast(F32), 1.0).then_inc(stacks_set, 1)
            dve.wait_ge(stacks_set, 5)
            V.memset(k_stack[96:98, :, 1, :].bitcast(F32), 0.0).then_inc(stacks_set, 1)
            V.memset(c_hi[:, D:D + 1].bitcast(F32), 1.0)
            V.memset(c_hi[:, D + 1:KVW].bitcast(F32), 0.0)
            V.memset(c_lo[:, D:KVW].bitcast(F32), 0.0)
            V.memset(b1_stat[:].bitcast(F32), 0.0).then_inc(dve_setup, 1)
            dve.wait_ge(w_loaded, W_COUNT)
            dve.wait_ge(pe_setup, 2)
            for k in range(KD):
                V.tensor_scalar(wqkvo_in[:, 0, k], wqkvo_in[:, 0, k], cols[:, 3, k:k + 1], SCALE, ALU.mult, ALU.mult)
                V.tensor_scalar(w1_in[:, k], w1_in[:, k], cols[:, 5, k:k + 1], None, ALU.mult)
            V.tensor_scalar(w2_in, w2_in, 0.5, None, ALU.mult).then_inc(dve_setup, 1)
            V.tensor_copy(wk_hi[:], wqkvo_in[:, 1])
            V.tensor_copy(wv_hi[:], wqkvo_in[:, 2])
            V.tensor_copy(wo_hi[:], wqkvo_in[:, 3]).then_inc(dve_setup, 1)
            dve.wait_ge(dve_setup, 3)
            V.tensor_copy(wq_hi[:], wqkvo_in[:, 0])
            V.tensor_copy(w1_hi[:], w1_in)
            V.tensor_copy(w2_hi[:], w2_in).then_inc(dve_setup, 1)
            V.tensor_tensor(wk_lo[:], wqkvo_in[:, 1], wk_hi[:].bitcast(F32), ALU.subtract)
            V.tensor_tensor(wv_lo[:], wqkvo_in[:, 2], wv_hi[:].bitcast(F32), ALU.subtract)
            V.tensor_tensor(wo_lo[:], wqkvo_in[:, 3], wo_hi[:].bitcast(F32), ALU.subtract)
            dve.wait_ge(dve_setup, 4)
            V.tensor_tensor(wq_lo[:], wqkvo_in[:, 0], wq_hi[:].bitcast(F32), ALU.subtract)
            V.tensor_tensor(w1_lo[:], w1_in, w1_hi[:].bitcast(F32), ALU.subtract)
            V.tensor_tensor(w2_lo[:], w2_in, w2_hi[:].bitcast(F32), ALU.subtract)
            dve.wait_ge(pe_setup, 4)
            V.tensor_tensor(bq_sum[:], X[:, 0, 0:KD], cols[:, 0], ALU.add)
            V.tensor_tensor(b1_row, S[0:1, 0:FF // BANK].rearrange("p n f -> p (n f)"), rows[:, 4 * D:], ALU.add)
            V.tensor_copy(bo_all[:], X[:, 1, 0:D])
            V.tensor_copy(b2_all[:], X[:, 2, 0:D])
            V.tensor_copy(gamma_all[:], X[:, 2, D:2 * D])
            V.tensor_copy(beta_all[:], X[:, 3, 0:D]).then_inc(dve_setup, 1)
            dve.wait_ge(dve_setup, 5)
            V.tensor_scalar(bq_col[:], bq_sum[:], SCALE, None, ALU.mult)
            V.tensor_copy(b1_stat[0:1], b1_row).then_inc(dve_setup, 1)
            dve.wait_ge(dve_setup, 6)
            V.tensor_tensor(b1_stat[32:33], b1_row, b1_stat[0:1].bitcast(F32), ALU.subtract).then_inc(dve_setup, 1)

            def norm_stats(i, src, stat_sem, mv_sem, b):
                for t in range(QT):
                    last = V.bn_stats(stats[:, i, t], src[:, t])
                last.then_inc(stat_sem, 1)
                dve.wait_ge(stat_sem, done(b))
                settled(dve)
                for t in range(QT):
                    last = V.bn_aggr(mv[:, i, t], stats[:, i, t])
                last.then_inc(mv_sem, 1)

            def norm_apply(i, dst, src):
                for t in range(QT):
                    last = V.tensor_scalar(dst[:, t], src[:, t], mv[:, i, t, 0:1], rstd[:, i, t:t + 1],
                                           ALU.subtract, ALU.mult)
                return last

            def lo_part(dst, src, hi):
                return V.tensor_tensor(dst, src, hi.bitcast(F32), ALU.subtract)

            def bank(b):
                return X[:, b].rearrange("p (k q) -> p k q", k=KD)

            def x_norm_stats(a):
                dve.wait_ge(x_loaded[a.slot], 16 * (a.half + 1))
                wait(dve, rstd1, number(a))
                norm_stats(0, xs[:, a.slot], stat1, mv1, a)

            def x_norm(a):
                dve.wait_ge(rstd1, done(a))
                wait(dve, xT_ps, number(a))
                norm_apply(0, xn, xs[:, a.slot]).then_inc(xn_set, 1)

            def maxima(a, t):
                dve.wait_ge(s_ps, done(a, QT, t + 1))
                if t == 0:
                    wait(dve, max_split, number(a))
                V.tensor_reduce(neg_max[:, t].rearrange("p (b h) -> p b h", b=4),
                                S[:, :, 0:4 * LK].rearrange("p b (h k) -> p b h k", h=4),
                                axis=AX.X, op=ALU.max, negate=True).then_inc(max_set, 1)

            def period(dve, a, d):
                if d is not None:
                    dve.wait_ge(cnT_hid, done(d))
                    lo_part(cnT_lo[:], bank(0), cnT_hi[:]).then_inc(cnT_split, 1)
                if a is not None:
                    if is_first(a):
                        x_norm_stats(a)
                        x_norm(a)
                    dve.wait_ge(xT_hid, done(a))
                    lo_part(xT_lo[:], bank(1), xT_hi[:]).then_inc(xT_split, 1)
                    dve.wait_ge(cT_hid, done(a))
                    lo_part(cT_lo[:], X[:, 2, 0:KD * LK].rearrange("p (k q) -> p k q", k=KD), cT_hi[:]).then_inc(cT_split, 1)
                    dve.wait_ge(c_exped, done(a))
                    wait(dve, kp_split, number(a))
                    V.scalar_tensor_tensor(out=k_phi[:], in0=c_exp[:], scalar=-1.0, in1=cs[:, a.slot], op0=ALU.add,
                                           op1=ALU.max).then_inc(k_phi_set, 1)
                if d is not None:
                    dve.wait_ge(wo_ps, done(d))
                    dve.wait_ge(x_bo_set, done(d))
                    V.tensor_tensor(x1[:], bank(3), x_bo[:, d.slot], ALU.add).then_inc(x1_set, 1)
                    dve.wait_ge(x1_set, done(d))
                    norm_stats(1, x1, stat2, mv2, d)
                if a is not None:
                    dve.wait_ge(k_phi_set, done(a))
                    wait(dve, kv_ps, KD * number(a))
                    V.tensor_copy(kp_hi[:], k_phi[:]).then_inc(kp_hid, 1)
                    dve.wait_ge(q_hid, done(a, KD))
                    for g in range(KD):
                        last = V.scalar_tensor_tensor(out=q_lo[:, g], in0=X[:, 0, g * LQ:(g + 1) * LQ],
                                                      scalar=bq_col[:, g:g + 1], in1=q_hi[:, g].bitcast(F32), op0=ALU.add,
                                                      op1=ALU.subtract)
                    last.then_inc(q_split, 1)
                if d is not None:
                    dve.wait_ge(rstd2, done(d))
                    wait(dve, hT_ps, number(d))
                    norm_apply(1, hn, x1).then_inc(hn_set, 1)
                if a is not None:
                    dve.wait_ge(k_hid, done(a, KD))
                    for g in range(KD):
                        last = V.scalar_tensor_tensor(out=k_lo[:, g], in0=X[:, 1, g * LK:(g + 1) * LK],
                                                      scalar=cols[:, 1, g:g + 1], in1=k_hi[:, g].bitcast(F32), op0=ALU.add,
                                                      op1=ALU.subtract)
                    last.then_inc(k_split, 1)
                    dve.wait_ge(kp_hid, done(a))
                    lo_part(kp_lo[:], k_phi[:], kp_hi[:]).then_inc(kp_split, 1)
                if d is not None:
                    dve.wait_ge(hT_hid, done(d))
                    lo_part(hT_lo[:], bank(3), hT_hi[:]).then_inc(hT_split, 1)
                if a is not None:
                    for c in range(KD):
                        dve.wait_ge(kv_hid, done(a, KD, c + 1))
                        lo_part(kv_lo[:, a.slot, c], X[:, c, 0:KVW], kv_hi[:, a.slot, c]).then_inc(kv_split, 1)

                def hidden(u):
                    dve.wait_ge(th_set, done(d, NU, u + 1))
                    wait(dve, a_split, NU * number(d))
                    V.scalar_tensor_tensor(out=act_f[:, u], in0=th[:, u % 2], scalar=1.0, in1=X[:, 2 + u % 2],
                                           op0=ALU.add, op1=ALU.mult).then_inc(act_set, 1)

                if d is not None:
                    hidden(0)
                    hidden(1)
                if a is not None:
                    maxima(a, 0)
                if d is not None:
                    hidden(2)
                    hidden(3)
                if a is not None:
                    if not is_last(a):
                        x_norm_stats(following(a))
                    maxima(a, 1)
                    dve.wait_ge(max_set, done(a, QT))
                    wait(dve, maxT_ps, number(a))
                    part = max_parts[:].rearrange("p t (a l m) -> p l t m a", a=2, l=2)
                    neg = neg_max[:].rearrange("p t (m a) -> p t m a", a=2)
                    for t in range(QT):
                        last = V.tensor_copy(part[:, 0, t], neg[:, t])
                    last.then_inc(max_hid, 1)
                    dve.wait_ge(max_hid, done(a))
                    for t in range(QT):
                        last = lo_part(part[:, 1, t], neg[:, t], part[:, 0, t])
                    last.then_inc(max_split, 1)
                    if not is_last(a):
                        x_norm(following(a))
                    dve.wait_ge(maxT_ps, done(a))
                    wait(dve, max_stacked, 16 * number(a))
                    V.tensor_copy(max_T[:], X[0:4 * PAIRS, 1, 0:LQ]).then_inc(maxT_set, 1)
                if d is not None:
                    dve.wait_ge(f2_ps, done(d))
                    dve.wait_ge(x1_b2_set, done(d))
                    V.tensor_tensor(x2, bank(0), x1_b2[:], ALU.add).then_inc(x2_set, 1)
                    dve.wait_ge(x2_exped, done(d))
                    wait(dve, qpT_ps, number(d))
                    V.scalar_tensor_tensor(out=q_phi.rearrange("p t e -> p (t e)"),
                                           in0=x2_exp.rearrange("p t e -> p (t e)"), scalar=-1.0,
                                           in1=x2.rearrange("p t e -> p (t e)"), op0=ALU.add,
                                           op1=ALU.max).then_inc(q_phi_set, 1)
                    dve.wait_ge(qpT_hid, done(d))
                    lo_part(qpT_lo[:], bank(1), qpT_hi[:]).then_inc(qpT_split, 1)
                if a is not None:
                    dve.wait_ge(aug_ps, done(a))
                    heads = S[:, 0:QT].rearrange("p t (h w) -> p t h w", w=VW)
                    V.reciprocal(den_inv[:], heads[:, :, :, DH]).then_inc(den_set, 1)
                    dve.wait_ge(den_set, done(a))
                    wait(dve, cnT_ps, number(a))
                    for t in range(QT):
                        last = V.tensor_tensor(cn[:, t].rearrange("p (h e) -> p h e", h=H), heads[:, t, :, 0:DH],
                                               den_inv[:, t, :, None].to_broadcast([P, H, DH]), ALU.mult)
                    last.then_inc(cn_set, 1)
                if d is not None:
                    dve.wait_ge(la_ps, done(d, QT))
                    V.tensor_scalar(z_den[:], S[:, 2:4, D], Z_EPS, None, ALU.add).then_inc(z_set, 1)
                    dve.wait_ge(z_set, done(d))
                    V.reciprocal(z_inv[:], z_den[:]).then_inc(z_inved, 1)
                    dve.wait_ge(z_inved, done(d))
                    wait(dve, y_set, number(d))
                    for t in range(QT):
                        last = V.scalar_tensor_tensor(out=x3[:, t], in0=S[:, 2 + t, 0:D], scalar=z_inv[:, t:t + 1],
                                                      in1=x2[:, t], op0=ALU.mult, op1=ALU.add)
                    last.then_inc(x3_set, 1)
                    dve.wait_ge(x3_set, done(d))
                    norm_stats(2, x3, stat3, mv3, d)

            periods(dve, period)

        @block.gpsimd
        def _(pool):
            G = nc.gpsimd
            G.memset(ident[:], 0.0).then_inc(ident_set, 1)
            pool.wait_ge(ident_set, 1)
            G.affine_select(out=ident[:], in_=ident[:], compare_op=ALU.not_equal, fill=1.0, base=0,
                            pattern=[[-1, P]], channel_multiplier=1).then_inc(ident_set, 1)
            pool.wait_ge(dve_setup, SETUP_STEPS)
            pool.wait_ge(dve_consts, 3)

            def inverse_deviation(i, mv_sem, var_sem, rstd_sem, b):
                pool.wait_ge(mv_sem, done(b))
                settled(pool)
                G.tensor_scalar(var_eps[:, i], mv[:, i, :, 1], 1.0, LN_EPS, ALU.mult, ALU.add).then_inc(var_sem, 1)
                pool.wait_ge(var_sem, done(b))
                G.tensor_tensor(rstd[:, i], var_eps[:, i], minus_half[:], ALU.pow).then_inc(rstd_sem, 1)

            def finish(d):
                inverse_deviation(2, mv3, var3, rstd3, d)
                pool.wait_ge(rstd3, done(d))
                G.tensor_tensor(mean_shift[:], mv[:, 2, :, 0], rstd[:, 2], ALU.mult).then_inc(shift_set, 1)
                pool.wait_ge(shift_set, done(d))
                settled(pool)
                for t in range(QT):
                    last = G.tensor_scalar(y[:, t], x3[:, t], rstd[:, 2, t:t + 1], mean_shift[:, t:t + 1],
                                           ALU.mult, ALU.subtract)
                last.then_inc(y_set, 1)
                pool.wait_ge(y_set, done(d))
                for t in range(QT):
                    last = G.tensor_tensor(yg[:, t], y[:, t], gamma_all[:], ALU.mult)
                last.then_inc(yg_set, 1)
                pool.wait_ge(yg_set, done(d))
                wait(pool, stored, 16 * number(d))
                for t in range(QT):
                    last = G.tensor_tensor(y_out[:, t], yg[:, t], beta_all[:], ALU.add)
                last.then_inc(y_out_set, 1)

            def period(pool, a, d):
                if a is not None:
                    if is_first(a):
                        inverse_deviation(0, mv1, var1, rstd1, a)
                    pool.wait_ge(c_loaded[a.slot], 16 * (a.half + 1))
                    wait(pool, c_exped, number(a))
                    settled(pool)
                    G.tensor_scalar(c_min[:], cs[:, a.slot], 0.0, 1.0, ALU.min, ALU.mult).then_inc(c_mined, 1)
                    wait(pool, kv_ps, KD * number(a))
                    settled(pool)
                    G.tensor_scalar(c_hi[:, 0:D], cs[:, a.slot], 1.0, 0.0, ALU.mult, ALU.add).then_inc(c_hid, 1)
                    pool.wait_ge(c_hid, done(a))
                    G.tensor_tensor(c_lo[:, 0:D], cs[:, a.slot], c_hi[:, 0:D].bitcast(F32), ALU.subtract).then_inc(c_split, 1)
                if d is not None:
                    inverse_deviation(1, mv2, var2, rstd2, d)
                    pool.wait_ge(x1_set, done(d))
                    wait(pool, x2_set, number(d))
                    for t in range(QT):
                        last = G.tensor_tensor(x1_b2[:, t], x1[:, t], b2_all[:], ALU.add)
                    last.then_inc(x1_b2_set, 1)
                    if not is_first(d):
                        finish(preceding(d))
                    for u in range(NU):
                        pool.wait_ge(a_hid, done(d, NU, u + 1))
                        if u == 0:
                            wait(pool, f2_ps, number(d))
                        G.tensor_tensor(a_lo[:, u], act_f[:, u], a_hi[:, u].bitcast(F32), ALU.subtract).then_inc(a_split, 1)
                if a is not None:
                    pool.wait_ge(x_loaded[a.slot], 16 * (a.half + 1))
                    wait(pool, x1_set, number(a) - 1)
                    for t in range(QT):
                        last = G.tensor_tensor(x_bo[:, a.slot, t], xs[:, a.slot, t], bo_all[:], ALU.add)
                    last.then_inc(x_bo_set, 1)
                    if not is_last(a):
                        inverse_deviation(0, mv1, var1, rstd1, following(a))
                if d is not None:
                    pool.wait_ge(x2_set, done(d))
                    wait(pool, x2_exped, number(d))
                    settled(pool)
                    G.tensor_scalar(x2_min, x2, 0.0, 1.0, ALU.min, ALU.mult).then_inc(x2_mined, 1)

            periods(pool, period)
            finish(Batch(B // 2 - 1, 1))


_INS = ['x', 'ctx_1024', 'L0_xattn_Wq', 'L0_xattn_bq', 'L0_xattn_Wk', 'L0_xattn_bk', 'L0_xattn_Wv', 'L0_xattn_bv',
        'L0_xattn_Wo', 'L0_xattn_bo', 'L0_xattn_W1', 'L0_xattn_b1', 'L0_xattn_W2', 'L0_xattn_b2', 'L0_xattn_ln_q_g',
        'L0_xattn_ln_q_b', 'L0_xattn_ln_ff_g', 'L0_xattn_ln_ff_b', 'L1_xattn_gamma', 'L1_xattn_beta']


def kernel(**inputs):
    import numpy as _np
    import concourse.bacc as _bacc
    from concourse import mybir as _mybir
    from concourse.bass_utils import run_bass_kernel_spmd as _run

    nc = _bacc.Bacc("TRN2", target_bir_lowering=False, num_devices=1)
    arrays, args = {}, []
    for name in _INS:
        a = _np.ascontiguousarray(inputs[name])
        arrays[f"in_{name}_dram"] = a
        args.append(nc.dram_tensor(f"in_{name}_dram", a.shape, _mybir.dt.from_np(a.dtype), kind="ExternalInput").ap())
    args.append(nc.dram_tensor("out_0_dram", inputs["x"].shape, _mybir.dt.float32, kind="ExternalOutput").ap())
    build(nc, *args)
    r = _run(nc, [arrays], core_ids=[0])
    return r.results[0]["out_0_dram"]
```

```python
from collections import namedtuple
from contextlib import ExitStack

import concourse.bass as bass
from concourse import mybir

F32 = mybir.dt.float32
F32R = mybir.dt.float32r
ALU = mybir.AluOpType
ACT = mybir.ActivationFunctionType
AX = mybir.AxisListType

Batch = namedtuple("Batch", "half slot")


def number(b):
    return 2 * b.half + b.slot


def following(b):
    return Batch(b.half, 1) if b.slot == 0 else Batch(b.half + 1, 0)


def preceding(b):
    return Batch(b.half, 0) if b.slot == 1 else Batch(b.half - 1, 1)


def done(b, per=1, k=None):
    return per * number(b) + (per if k is None else k)


def wait(eng, sem, count):
    if not isinstance(count, int) or count > 0:
        eng.wait_ge(sem, count)


def build(nc, x, ctx, Wq, bq, Wk, bk, Wv, bv, Wo, bo, W1, b1, W2, b2,
          ln_q_g, ln_q_b, ln_ff_g, ln_ff_b, gamma, beta, out):
    P = 128
    B, LQ, D = x.shape
    LK = ctx.shape[1]
    FF = W1.shape[1]
    H = 16
    DH = D // H
    QT = LQ // P
    KD = D // P
    PAIRS = H // 2
    NU = FF // (2 * P)
    BANK = 512
    VW = 32
    KVW = D + 2
    PARTS = 3
    LN_EPS = 1e-5
    Z_EPS = 1e-6
    SCALE = float(DH) ** -0.5
    assert QT == 2 and KD == 2 and B % 2 == 0 and B >= 4 and QT * D == BANK and SCALE == 0.25

    es = ExitStack()
    with es:
        def sb(name, shape, dt=F32):
            return es.enter_context(nc.sbuf_tensor(name, shape, dt))

        def sem(name):
            return es.enter_context(nc.semaphore(name))

        wq_hi, wq_lo = sb("wq_hi", [P, KD, D], F32R), sb("wq_lo", [P, KD, D], F32R)
        wk_hi, wk_lo = sb("wk_hi", [P, KD, D], F32R), sb("wk_lo", [P, KD, D], F32R)
        wv_hi, wv_lo = sb("wv_hi", [P, KD, D], F32R), sb("wv_lo", [P, KD, D], F32R)
        wo_hi, wo_lo = sb("wo_hi", [P, KD, D], F32R), sb("wo_lo", [P, KD, D], F32R)
        w1_hi, w1_lo = sb("w1_hi", [P, KD, FF], F32R), sb("w1_lo", [P, KD, FF], F32R)
        w2_hi, w2_lo = sb("w2_hi", [P, FF // P, D], F32R), sb("w2_lo", [P, FF // P, D], F32R)
        cols = sb("cols", [P, 7, KD])
        bq_sum, bq_col = sb("bq_sum", [P, KD]), sb("bq_col", [P, KD])
        b1_stat = sb("b1_stat", [P, FF], F32R)
        ones = sb("ones", [P, LQ])
        ones_r = sb("ones_r", [P, LQ], F32R)
        bv_wide = sb("bv_wide", [P, KD, P])
        bo_all, b2_all = sb("bo_all", [P, D]), sb("b2_all", [P, D])
        gamma_all, beta_all = sb("gamma_all", [P, D]), sb("beta_all", [P, D])
        ident = sb("ident", [P, P])
        minus_half = sb("minus_half", [P, QT])

        xs = sb("xs", [P, 2, QT, D])
        cs = sb("cs", [LK, 2, D])
        x_bo = sb("x_bo", [P, QT, D])
        stats = sb("stats", [P, 3, QT, 6])
        mv = sb("mv", [P, 3, QT, 2])
        var_eps = sb("var_eps", [P, 3, QT])
        rstd = sb("rstd", [P, 3, QT])
        xn = sb("xn", [P, QT, D])
        xT_hi, xT_lo = sb("xT_hi", [P, KD, LQ], F32R), sb("xT_lo", [P, KD, LQ], F32R)
        cT_hi, cT_lo = sb("cT_hi", [P, KD, LK], F32R), sb("cT_lo", [P, KD, LK], F32R)
        q_hi, q_lo = sb("q_hi", [P, KD, LQ], F32R), sb("q_lo", [P, KD, LQ], F32R)
        k_hi, k_lo = sb("k_hi", [P, KD, LK], F32R), sb("k_lo", [P, KD, LK], F32R)
        q_stack = sb("q_stack", [P, PAIRS, LQ], F32R)
        k_stack = sb("k_stack", [P, 2, PAIRS, LK], F32R)
        v_aug = sb("v_aug", [LK, 2, H, VW])
        neg_max = sb("neg_max", [P, QT, H])
        max_parts = sb("max_parts", [P, QT, 4 * PAIRS], F32R)
        max_T = sb("max_T", [4 * PAIRS, LQ], F32R)
        probs = sb("probs", [LK, H, LQ])
        aug = sb("aug", [P, H // 4, LQ])
        den_inv = sb("den_inv", [P, QT, H])
        cn = sb("cn", [P, QT, D])
        cnT_hi, cnT_lo = sb("cnT_hi", [P, KD, LQ], F32R), sb("cnT_lo", [P, KD, LQ], F32R)
        c_min, c_exp, k_phi = sb("c_min", [LK, D]), sb("c_exp", [LK, D]), sb("k_phi", [LK, D])
        c_hi, c_lo = sb("c_hi", [LK, KVW], F32R), sb("c_lo", [LK, KVW], F32R)
        kp_hi, kp_lo = sb("kp_hi", [LK, D], F32R), sb("kp_lo", [LK, D], F32R)
        kv_hi, kv_lo = sb("kv_hi", [P, 2, KD, KVW], F32R), sb("kv_lo", [P, 2, KD, KVW], F32R)
        x1, x1_b2, hn = sb("x1", [P, QT, D]), sb("x1_b2", [P, QT, D]), sb("hn", [P, QT, D])
        hT_hi, hT_lo = sb("hT_hi", [P, KD, LQ], F32R), sb("hT_lo", [P, KD, LQ], F32R)
        th = sb("th", [P, 2, BANK])
        act_f = sb("act_f", [P, NU, BANK])
        a_hi, a_lo = sb("a_hi", [P, NU, BANK], F32R), sb("a_lo", [P, NU, BANK], F32R)
        x2_tiles = sb("x2_tiles", [P, 4, QT, D])
        x2, x2_min, x2_exp, q_phi = (x2_tiles[:, i] for i in range(4))
        qpT_hi, qpT_lo = sb("qpT_hi", [P, KD, LQ], F32R), sb("qpT_lo", [P, KD, LQ], F32R)
        z_den, z_inv = sb("z_den", [P, QT]), sb("z_inv", [P, QT])
        x3_tiles = sb("x3_tiles", [P, 4, QT, D])
        x3, y, yg, y_out = (x3_tiles[:, i] for i in range(4))
        mean_rstd, mean_shift = sb("mean_rstd", [P, QT]), sb("mean_shift", [P, QT])

        wq_raw = hn
        rows = probs[0:1].rearrange("o h q -> o (h q)")[:, 0:4 * D + FF]
        b1_row = th[0:1].rearrange("o i n -> o (i n)")
        w1_in = act_f[:].rearrange("p u (i n) -> p (u i n)", i=2).rearrange("p (k n) -> p k n", k=KD)
        w2_in = x2_tiles[:].rearrange("p i t e -> p (i t e)").rearrange("p (c n) -> p c n", n=D)
        wqkvo_in = x3_tiles[:].rearrange("p i t e -> p (i t e)").rearrange("p (i k n) -> p i k n", i=4, k=KD)

        S = es.enter_context(nc.psum_tensor("S", [P, 4, BANK], F32))
        X = es.enter_context(nc.psum_tensor("X", [P, 4, BANK], F32))

        w_loaded, small_loaded = sem("w_loaded"), sem("small_loaded")
        passed, dve_consts, dve_setup, pe_setup, stacks_set, ident_set = (
            sem(n) for n in ("passed", "dve_consts", "dve_setup", "pe_setup", "stacks_set", "ident_set"))
        x_loaded = [sem(f"x_loaded{i}") for i in range(2)]
        c_loaded = [sem(f"c_loaded{i}") for i in range(2)]
        q_stacked, k_stacked, max_stacked, stored = (sem(n) for n in ("q_stacked", "k_stacked", "max_stacked", "stored"))
        xT_ps, cT_ps, q_ps, k_ps, v_ps, kv_ps, s_ps, maxT_ps, st_ps, pv_ps, aug_ps = (
            sem(n) for n in ("xT_ps", "cT_ps", "q_ps", "k_ps", "v_ps", "kv_ps", "s_ps", "maxT_ps", "st_ps", "pv_ps", "aug_ps"))
        cnT_ps, wo_ps, hT_ps, f1_ps, f2_ps, qpT_ps, la_ps = (
            sem(n) for n in ("cnT_ps", "wo_ps", "hT_ps", "f1_ps", "f2_ps", "qpT_ps", "la_ps"))
        xT_hid, cT_hid, q_hid, k_hid, v_copied, c_exped, kv_hid, probs_set, aug_set = (
            sem(n) for n in ("xT_hid", "cT_hid", "q_hid", "k_hid", "v_copied", "c_exped", "kv_hid", "probs_set", "aug_set"))
        cnT_hid, hT_hid, th_set, a_hid, x2_exped, qpT_hid = (
            sem(n) for n in ("cnT_hid", "hT_hid", "th_set", "a_hid", "x2_exped", "qpT_hid"))
        stat1, mv1, xn_set, xT_split, cT_split, q_split, k_split, k_phi_set, kp_hid, kp_split, kv_split = (
            sem(n) for n in ("stat1", "mv1", "xn_set", "xT_split", "cT_split", "q_split", "k_split", "k_phi_set", "kp_hid",
                             "kp_split", "kv_split"))
        max_set, max_hid, max_split, maxT_set, den_set, cn_set, cnT_split = (
            sem(n) for n in ("max_set", "max_hid", "max_split", "maxT_set", "den_set", "cn_set", "cnT_split"))
        x1_set, stat2, mv2, hn_set, hT_split, act_set, x2_set, q_phi_set, qpT_split, z_set, z_inved, x3_set, stat3, mv3 = (
            sem(n) for n in ("x1_set", "stat2", "mv2", "hn_set", "hT_split", "act_set", "x2_set", "q_phi_set", "qpT_split",
                             "z_set", "z_inved", "x3_set", "stat3", "mv3"))
        c_mined, c_hid, c_split, x_bo_set, var1, rstd1, var2, rstd2, x1_b2_set, a_split, x2_mined, var3, rstd3 = (
            sem(n) for n in ("c_mined", "c_hid", "c_split", "x_bo_set", "var1", "rstd1", "var2", "rstd2", "x1_b2_set",
                             "a_split", "x2_mined", "var3", "rstd3"))
        mean_set, shift_set, y_set, yg_set, y_out_set = (sem(n) for n in ("mean_set", "shift_set", "y_set", "yg_set", "y_out_set"))

        W_COUNT, SMALL_COUNT, SETUP_STEPS = 16 * 6, 16 * 14, 7

        block = es.enter_context(nc.Block())

        def periods(eng, period):
            def line(n):
                return [Batch(m // 2, m % 2) if 0 <= m < B else None for m in (n, n - 1, n - 2, n - 3)]

            for n in range(4):
                period(eng, *line(n))
            with eng.Fori(2, B // 2) as j:
                period(eng, Batch(j, 0), Batch(j - 1, 1), Batch(j - 1, 0), Batch(j - 2, 1))
                period(eng, Batch(j, 1), Batch(j, 0), Batch(j - 1, 1), Batch(j - 1, 0))
            for n in range(B, B + 3):
                period(eng, *line(n))

        def settled(eng):
            eng.sem_inc(passed)

        def is_first(b):
            return isinstance(b.half, int) and b == Batch(0, 0)

        @block.sync
        def _(sp):
            def load(b):
                for sem_ in (x_bo_set, cT_ps, k_phi_set, c_split):
                    wait(sp, sem_, number(b) - 1)
                sp.dma_start(xs[:, b.slot], x[bass.ds(number(b), 1)].rearrange("b (t p) d -> p (b t) d", p=P)
                             ).then_inc(x_loaded[b.slot], 16)
                sp.dma_start(cs[:, b.slot], ctx[bass.ds(number(b), 1)].rearrange("b k d -> k (b d)")
                             ).then_inc(c_loaded[b.slot], 16)

            load(Batch(0, 0))
            load(Batch(0, 1))
            for i, v in enumerate((bq, bk)):
                for g in range(KD):
                    sp.dma_start(cols[:, i, g:g + 1], v[g * P:(g + 1) * P].rearrange("(j r o) -> r j o", r=2 * DH, o=1),
                                 allow_slow_non_contiguous=True).then_inc(small_loaded, 16)
            for i, v in ((2, bv), (3, ln_q_g), (4, ln_q_b), (5, ln_ff_g), (6, ln_ff_b)):
                sp.dma_start(cols[:, i], v.rearrange("(k p) -> p k", p=P), allow_slow_non_contiguous=True).then_inc(small_loaded, 16)
            for i, v in enumerate((bo, b2, gamma, beta)):
                sp.dma_start(rows[:, i * D:(i + 1) * D], v.rearrange("(a d) -> a d", a=1)).then_inc(small_loaded, 16)
            sp.dma_start(rows[:, 4 * D:], b1.rearrange("(a d) -> a d", a=1)).then_inc(small_loaded, 16)
            for i, w in enumerate((Wq, Wk, Wv, Wo)):
                sp.dma_start(wqkvo_in[:, i], w.rearrange("(k p) n -> p k n", p=P)).then_inc(w_loaded, 16)
            sp.dma_start(w1_in, W1.rearrange("(k p) n -> p k n", p=P)).then_inc(w_loaded, 16)
            sp.dma_start(w2_in, W2.rearrange("(k p) n -> p k n", p=P)).then_inc(w_loaded, 16)

            def store(d):
                sp.wait_ge(y_out_set, done(d))
                sp.dma_start(out[bass.ds(number(d), 1)].rearrange("b (t p) d -> p (b t) d", p=P), y_out
                             ).then_inc(stored, 16)

            def period(sp, f, a, d, e):
                if f is not None and not (isinstance(f.half, int) and f.half == 0):
                    load(f)
                if a is not None:
                    sp.wait_ge(maxT_set, done(a))
                    sp.dma_start(q_stack[96:100].bitcast(F32), max_T[:].bitcast(F32)).then_inc(max_stacked, 16)
                if e is not None:
                    store(e)
                if f is not None:
                    if is_first(f):
                        sp.wait_ge(stacks_set, 6)
                    if a is not None:
                        sp.wait_ge(st_ps, done(a, PAIRS))
                        settled(sp)
                    sp.wait_ge(k_split, done(f))
                    settled(sp)
                    for part, src in enumerate((k_hi, k_lo, k_hi)):
                        for ab in range(2):
                            r = 32 * part + DH * ab
                            sp.dma_start(k_stack[r:r + DH, ab].bitcast(F32), src[64 * ab:64 * ab + 64].bitcast(F32)
                                         ).then_inc(k_stacked, 16)
                    sp.wait_ge(q_split, done(f))
                    for part, src in enumerate((q_hi, q_hi, q_lo)):
                        sp.dma_start(q_stack[32 * part:32 * part + 32].bitcast(F32), src[:].bitcast(F32)
                                     ).then_inc(q_stacked, 16)

            periods(sp, period)
            sp.wait_ge(stored, 16 * B)

        K_DMAS, Q_DMAS = PARTS * 2, PARTS

        @block.tensor
        def _(pe):
            def split_mm(out_, stat, mov, n):
                parts = [(c, s, m) for c in range(n) for s, m in ((0, 1), (1, 0), (0, 0))]
                for i, (c, s, m) in enumerate(parts):
                    last = nc.tensor.matmul(out_, stat(c, s), mov(c, m), start=(i == 0), stop=(i == len(parts) - 1))
                return last

            pe.wait_ge(w_loaded, W_COUNT)
            pe.wait_ge(small_loaded, SMALL_COUNT)
            pe.wait_ge(dve_consts, 4)
            for m in range(KD):
                for k in range(KD):
                    last = nc.tensor.matmul(X[:, 0, m:m + 1], wq_raw[:, k, m * P:(m + 1) * P], cols[:, 4, k:k + 1],
                                            start=(k == 0), stop=(k == KD - 1))
            last.then_inc(pe_setup, 1)
            for n in range(FF // BANK):
                for k in range(KD):
                    last = nc.tensor.matmul(S[0:1, n, :], cols[:, 6, k:k + 1], w1_in[:, k, n * BANK:(n + 1) * BANK],
                                            start=(k == 0), stop=(k == KD - 1))
            last.then_inc(pe_setup, 1)
            for k in range(KD):
                nc.tensor.matmul(X[:, 1, 0:D], bv_wide[:, k], wqkvo_in[:, 3, k], start=(k == 0), stop=False)
            nc.tensor.matmul(X[:, 1, 0:D], ones[0:1, 0:P], rows[:, 0:D], start=False, stop=True).then_inc(pe_setup, 1)
            for i in range(1, 4):
                bank = (X[:, 2, 0:D], X[:, 2, D:2 * D], X[:, 3, 0:D])[i - 1]
                last = nc.tensor.matmul(bank, ones[0:1, 0:P], rows[:, i * D:(i + 1) * D], start=True, stop=True)
            last.then_inc(pe_setup, 1)
            pe.wait_ge(ident_set, 2)
            pe.wait_ge(dve_setup, SETUP_STEPS)
            pe.wait_ge(stacks_set, 6)

            def rows_to_columns(out_, src):
                for k in range(KD):
                    for t in range(QT):
                        last = nc.tensor.transpose(out_[:, k * LQ + t * P:k * LQ + (t + 1) * P],
                                                   src[:, t, k * P:(k + 1) * P], ident[:])
                return last


            def linear_attention(e, d):
                pe.wait_ge(qpT_split, done(e))
                pe.wait_ge(kv_split, done(e, KD))
                if d is not None:
                    pe.wait_ge(probs_set, done(d, PAIRS))
                for t in range(QT):
                    split_mm(S[:, 2 + t, 0:KVW], lambda c, s: (qpT_hi, qpT_lo)[s][:, c, t * P:(t + 1) * P],
                             lambda c, m: (kv_hi, kv_lo)[m][:, e.slot, c], KD).then_inc(la_ps, 1)

            def attention_columns(d):
                pe.wait_ge(cn_set, done(d))
                wait(pe, x2_set, number(d))
                rows_to_columns(X[:, 0], cn).then_inc(cnT_ps, 1)

            def linear_state(a):
                pe.wait_ge(kp_split, done(a))
                pe.wait_ge(c_split, done(a))
                wait(pe, qpT_split, number(a) - 1)
                pe.wait_ge(xT_split, done(a))
                wait(pe, aug_set, 2 * number(a))
                for c in range(KD):
                    split_mm(X[:, 1 + c, 0:KVW], lambda _, s: (kp_hi, kp_lo)[s][:, c * P:(c + 1) * P],
                             lambda _, m: (c_hi, c_lo)[m][:], 1).then_inc(kv_ps, 1)

            def project_o(d):
                pe.wait_ge(cnT_split, done(d))
                for t in range(QT):
                    last = split_mm(X[:, 0, t * D:(t + 1) * D], lambda c, s: (cnT_hi, cnT_lo)[s][:, c, t * P:(t + 1) * P],
                                    lambda c, m: (wo_hi, wo_lo)[m][:, c], KD)
                last.then_inc(wo_ps, 1)

            def context_columns(f):
                pe.wait_ge(c_loaded[f.slot], 16 * (f.half + 1))
                wait(pe, aug_set, 2 * (number(f) - 1))
                for k in range(KD):
                    last = nc.tensor.transpose(X[:, 3, k * LK:(k + 1) * LK], cs[:, f.slot, k * P:(k + 1) * P],
                                               ident[0:LK, 0:LK])
                last.then_inc(cT_ps, 1)

            def project_v(f):
                pe.wait_ge(cT_split, done(f))
                split_mm(X[0:LK, 3, 0:D], lambda c, s: (cT_hi, cT_lo)[s][:, c],
                         lambda c, m: (wv_hi, wv_lo)[m][:, c], KD).then_inc(v_ps, 1)

            def project_k(f, a):
                if a is not None:
                    pe.wait_ge(kv_split, done(a, KD, 1))
                for g in range(KD):
                    last = split_mm(X[:, 1, g * LK:(g + 1) * LK],
                                    lambda c, s: (wk_hi, wk_lo)[s][:, c, g * P:(g + 1) * P],
                                    lambda c, m: (cT_hi, cT_lo)[m][:, c], KD)
                last.then_inc(k_ps, 1)

            def hidden_columns(d):
                pe.wait_ge(hn_set, done(d))
                rows_to_columns(X[:, 0], hn).then_inc(hT_ps, 1)

            def x_columns(f):
                pe.wait_ge(xn_set, done(f))
                pe.wait_ge(k_split, done(f))
                rows_to_columns(X[:, 1], xn).then_inc(xT_ps, 1)

            def project_q(f, d):
                pe.wait_ge(xT_split, done(f))
                if d is not None:
                    pe.wait_ge(hT_split, done(d))
                for g in range(KD):
                    last = split_mm(X[:, 0, g * LQ:(g + 1) * LQ],
                                    lambda c, s: (wq_hi, wq_lo)[s][:, c, g * P:(g + 1) * P],
                                    lambda c, m: (xT_hi, xT_lo)[m][:, c], KD)
                last.then_inc(q_ps, 1)

            def scores(a, e, t):
                if t == 0:
                    pe.wait_ge(k_stacked, 16 * K_DMAS * done(a))
                    pe.wait_ge(q_stacked, 16 * Q_DMAS * done(a))
                    wait(pe, cn_set, number(a))
                    if e is not None:
                        pe.wait_ge(x3_set, done(e))
                else:
                    pe.wait_ge(max_set, done(a, 2 * QT, 2 * t))
                for p in range(PAIRS):
                    last = nc.tensor.matmul(S[:, p // 2, (p % 2) * 2 * LK:(p % 2 + 1) * 2 * LK],
                                            q_stack[0:96, p, t * P:(t + 1) * P],
                                            k_stack[0:96, :, p], start=True, stop=True)
                last.then_inc(s_ps, 1)

            def max_columns(a, f):
                pe.wait_ge(max_split, done(a))
                if f is not None:
                    pe.wait_ge(xT_split, done(f))
                else:
                    pe.wait_ge(kv_split, done(a, KD, 1))
                for t in range(QT):
                    last = nc.tensor.transpose(X[0:4 * PAIRS, 1, t * P:(t + 1) * P], max_parts[:, t].bitcast(F32), ident[:])
                last.then_inc(maxT_ps, 1)

            def ffn_up(d, f, a, u):
                if u == 0:
                    pe.wait_ge(hT_split, done(d))
                    if a is not None:
                        pe.wait_ge(kv_split, done(a, KD))
                    pe.wait_ge(aug_set, done(d, 2))
                if u == 1 and f is not None:
                    pe.wait_ge(v_copied, done(f))
                if u >= 2:
                    pe.wait_ge(act_set, done(d, NU, u - 1))
                for i in range(2):
                    m = 2 * u + i
                    o = X[:, 2 + u % 2, i * LQ:(i + 1) * LQ]
                    nc.tensor.matmul(o, b1_stat[:, m * P:(m + 1) * P], ones_r[:], start=True, stop=False)
                    parts = [(c, s, v) for c in range(KD) for s, v in ((0, 1), (1, 0), (0, 0))]
                    for n, (c, s, v) in enumerate(parts):
                        last = nc.tensor.matmul(o, (w1_hi, w1_lo)[s][:, c, m * P:(m + 1) * P], (hT_hi, hT_lo)[v][:, c],
                                                start=False, stop=(n == len(parts) - 1))
                last.then_inc(f1_ps, 1)

            def ffn_down(d, f, t):
                if t == 0 and f is not None:
                    pe.wait_ge(q_split, done(f))
                n = 0
                for u in range(NU):
                    if t == 0:
                        pe.wait_ge(a_split, done(d, NU, u + 1))
                    for i in range(2):
                        for s, v in ((0, 1), (1, 0), (0, 0)):
                            lo = i * LQ + t * P
                            last = nc.tensor.matmul(X[:, 0, t * D:(t + 1) * D], (a_hi, a_lo)[s][:, u, lo:lo + P],
                                                    (w2_hi, w2_lo)[v][:, 2 * u + i], start=(n == 0),
                                                    stop=(n == NU * 2 * PARTS - 1))
                            n += 1
                if t == QT - 1:
                    last.then_inc(f2_ps, 1)

            def scores_T(a, p):
                if p == 0:
                    pe.wait_ge(max_stacked, 16 * done(a))
                    pe.wait_ge(max_set, done(a, 2 * QT))
                if p >= 4:
                    pe.wait_ge(probs_set, done(a, PAIRS, p - 3))
                for ab in range(2):
                    last = nc.tensor.matmul(S[0:LK, p % 4, ab * LQ:(ab + 1) * LQ], k_stack[0:100, ab, p],
                                            q_stack[0:100, p], start=True, stop=True)
                last.then_inc(st_ps, 1)

            def attend(a, G):
                pe.wait_ge(probs_set, done(a, PAIRS, 2 * G + 2))
                if G == 0:
                    pe.wait_ge(v_copied, done(a))
                for c in range(4):
                    h = 4 * G + c
                    last = nc.tensor.matmul(X[32 * c:32 * c + VW, 2 + G // 2, (G % 2) * LQ:(G % 2 + 1) * LQ],
                                            v_aug[:, a.slot, h], probs[:, h], start=True, stop=True)
                if G % 2 == 1:
                    last.then_inc(pv_ps, 1)

            def q_phi_columns(d, a):
                pe.wait_ge(q_phi_set, done(d))
                if a is not None:
                    pe.wait_ge(maxT_set, done(a))
                rows_to_columns(X[:, 1], q_phi).then_inc(qpT_ps, 1)

            def attention_rows(a):
                pe.wait_ge(aug_set, done(a, 2))
                pe.wait_ge(probs_set, done(a, PAIRS))
                for t in range(QT):
                    for G in range(H // 4):
                        last = nc.tensor.transpose(S[:, t, G * P:(G + 1) * P], aug[:, G, t * P:(t + 1) * P], ident[:])
                last.then_inc(aug_ps, 1)

            def period(pe, f, a, d, e):
                if e is not None:
                    linear_attention(e, d)
                if d is not None:
                    attention_columns(d)
                if a is not None:
                    linear_state(a)
                if d is not None:
                    project_o(d)
                if f is not None:
                    context_columns(f)
                    project_v(f)
                    project_k(f, a)
                if d is not None:
                    hidden_columns(d)
                if a is not None:
                    scores(a, e, 0)
                if d is not None:
                    ffn_up(d, f, a, 0)
                if f is not None:
                    x_columns(f)
                if d is not None:
                    ffn_up(d, f, a, 1)
                if a is not None:
                    scores(a, e, 1)
                if d is not None:
                    ffn_up(d, f, a, 2)
                    ffn_up(d, f, a, 3)
                if f is not None:
                    project_q(f, d)
                if a is not None:
                    max_columns(a, f)
                if d is not None:
                    ffn_down(d, f, 0)
                    ffn_down(d, f, 1)
                if a is not None:
                    for p in range(4):
                        scores_T(a, p)
                    if d is not None:
                        pe.wait_ge(act_set, done(d, NU))
                    elif f is not None:
                        pe.wait_ge(v_copied, done(f))
                    attend(a, 0)
                    scores_T(a, 4)
                    scores_T(a, 5)
                    attend(a, 1)
                    scores_T(a, 6)
                    scores_T(a, 7)
                    attend(a, 2)
                    attend(a, 3)
                if d is not None:
                    q_phi_columns(d, a)
                if a is not None:
                    attention_rows(a)

            periods(pe, period)

        @block.scalar
        def _(act):
            def columns_hi(dst, bank):
                return nc.scalar.copy(dst[:], X[:, bank].rearrange("p (k q) -> p k q", k=KD))

            def period(act, f, a, d, e):
                if d is not None:
                    act.wait_ge(cnT_ps, done(d))
                    wait(act, wo_ps, number(d))
                    columns_hi(cnT_hi, 0).then_inc(cnT_hid, 1)
                if a is not None:
                    wait(act, la_ps, QT * (number(a) - 1))
                    for c in range(KD):
                        act.wait_ge(kv_ps, done(a, KD, c + 1))
                        nc.scalar.copy(kv_hi[:, a.slot, c], X[:, 1 + c, 0:KVW]).then_inc(kv_hid, 1)
                if f is not None:
                    act.wait_ge(cT_ps, done(f))
                    wait(act, k_ps, number(f))
                    nc.scalar.copy(cT_hi[:], X[:, 3, 0:KD * LK].rearrange("p (k q) -> p k q", k=KD)).then_inc(cT_hid, 1)
                    act.wait_ge(c_loaded[f.slot], 16 * (f.half + 1))
                    nc.scalar.activation(c_min[:], cs[:, f.slot], ACT.Relu, scale=-1.0).then_inc(c_mined, 1)
                    act.wait_ge(c_mined, done(f))
                    wait(act, k_phi_set, number(f))
                    nc.scalar.activation(c_exp[:], c_min[:], ACT.Exp, scale=-1.0).then_inc(c_exped, 1)
                    act.wait_ge(v_ps, done(f))
                    wait(act, pv_ps, 2 * (number(f) - 1))
                    for g in range(KD):
                        last = nc.scalar.copy(
                            v_aug[:, f.slot].rearrange("k (j g a) w -> k g j a w", g=KD, a=2)[:, g, :, :, 0:DH],
                            X[0:LK, 3, g * P:(g + 1) * P].rearrange("k (j a e) -> k j a e", a=2, e=DH))
                    last.then_inc(v_copied, 1)
                    act.wait_ge(k_ps, done(f))
                    wait(act, k_stacked, 16 * K_DMAS * number(f))
                    for g in range(KD):
                        nc.scalar.activation(k_hi[:, g], X[:, 1, g * LK:(g + 1) * LK], ACT.Identity,
                                             bias=cols[:, 1, g:g + 1]).then_inc(k_hid, 1)
                if d is not None:
                    act.wait_ge(hT_ps, done(d))
                    wait(act, f1_ps, NU * number(d))
                    columns_hi(hT_hi, 0).then_inc(hT_hid, 1)

                def hidden_hi(u):
                    act.wait_ge(act_set, done(d, NU, u + 1))
                    if u == 0:
                        wait(act, f2_ps, number(d))
                    nc.scalar.copy(a_hi[:, u], act_f[:, u]).then_inc(a_hid, 1)

                def gate(u):
                    act.wait_ge(f1_ps, done(d, NU, u + 1))
                    wait(act, act_set, done(d, NU, u - 1))
                    nc.scalar.activation(th[:, u % 2], X[:, 2 + u % 2], ACT.Tanh, scale=0.5).then_inc(th_set, 1)

                if d is not None:
                    gate(0)
                if f is not None:
                    act.wait_ge(xT_ps, done(f))
                    wait(act, q_ps, number(f))
                    columns_hi(xT_hi, 1).then_inc(xT_hid, 1)
                if d is not None:
                    hidden_hi(0)
                    for u in range(1, NU):
                        gate(u)
                        hidden_hi(u)
                if f is not None:
                    act.wait_ge(q_ps, done(f))
                    wait(act, q_stacked, 16 * Q_DMAS * number(f))
                    for g in range(KD):
                        nc.scalar.activation(q_hi[:, g], X[:, 0, g * LQ:(g + 1) * LQ], ACT.Identity,
                                             bias=bq_col[:, g:g + 1]).then_inc(q_hid, 1)

                def exponentiate(p):
                    act.wait_ge(st_ps, done(a, PAIRS, p + 1))
                    nc.scalar.activation(probs[:, 2 * p:2 * p + 2], S[0:LK, p % 4].rearrange("k (h q) -> k h q", h=2),
                                         ACT.Exp).then_inc(probs_set, 1)

                if a is not None:
                    wait(act, pv_ps, 2 * number(a))
                    for p in range(4):
                        exponentiate(p)
                if d is not None:
                    act.wait_ge(x2_mined, done(d))
                    wait(act, q_phi_set, number(d))
                    nc.scalar.activation(x2_exp, x2_min, ACT.Exp).then_inc(x2_exped, 1)

                def copy_attention(i):
                    act.wait_ge(pv_ps, done(a, 2, i + 1))
                    nc.scalar.copy(aug[:, 2 * i:2 * i + 2], X[:, 2 + i].rearrange("p (g q) -> p g q", g=2)
                                   ).then_inc(aug_set, 1)

                if a is not None:
                    for p in range(4, PAIRS):
                        exponentiate(p)
                    wait(act, aug_ps, number(a))
                    copy_attention(0)
                    copy_attention(1)
                if d is not None:
                    act.wait_ge(qpT_ps, done(d))
                    wait(act, la_ps, QT * number(d))
                    columns_hi(qpT_hi, 1).then_inc(qpT_hid, 1)

            act.wait_ge(dve_setup, SETUP_STEPS)
            act.wait_ge(stacks_set, 6)
            act.wait_ge(small_loaded, SMALL_COUNT)
            periods(act, period)

        @block.vector
        def _(dve):
            V = nc.vector
            V.memset(ones[:], 1.0).then_inc(dve_consts, 1)
            dve.wait_ge(dve_consts, 1)
            dve.wait_ge(small_loaded, SMALL_COUNT)
            for k in range(KD):
                last = V.tensor_scalar(bv_wide[:, k], ones[:, 0:P], cols[:, 2, k:k + 1], None, ALU.mult)
            last.then_inc(dve_consts, 1)
            V.memset(minus_half[:], -0.5).then_inc(dve_consts, 1)
            def chunks(w, order):
                return [w[:, k].rearrange(order, g=KD, r=2 * DH) for k in range(KD)]

            raw, permuted = "p (g j r) -> p g r j", "p (g r j) -> p g r j"
            dve.wait_ge(w_loaded, W_COUNT)
            for dst, src in zip(chunks(wq_raw, permuted), chunks(wqkvo_in[:, 0], raw)):
                last = V.tensor_copy(dst, src)
            last.then_inc(dve_consts, 1)
            V.memset(k_stack[:].bitcast(F32), 0.0).then_inc(stacks_set, 1)
            V.memset(v_aug[:], 0.0).then_inc(stacks_set, 1)
            V.tensor_copy(ones_r[:], ones[:])
            dve.wait_ge(stacks_set, 2)
            V.memset(v_aug[:, :, :, DH:DH + 1], 1.0).then_inc(stacks_set, 1)
            V.memset(k_stack[96:98, 0].bitcast(F32), 1.0).then_inc(stacks_set, 1)
            V.memset(k_stack[96:100, 1].bitcast(F32), 1.0).then_inc(stacks_set, 1)
            dve.wait_ge(stacks_set, 5)
            V.memset(k_stack[96:98, 1].bitcast(F32), 0.0).then_inc(stacks_set, 1)
            V.memset(c_hi[:, D:D + 1].bitcast(F32), 1.0)
            V.memset(c_hi[:, D + 1:KVW].bitcast(F32), 0.0)
            V.memset(c_lo[:, D:KVW].bitcast(F32), 0.0)
            V.memset(b1_stat[:].bitcast(F32), 0.0).then_inc(dve_setup, 1)
            dve.wait_ge(dve_consts, 4)
            dve.wait_ge(pe_setup, 2)
            for k in range(KD):
                V.tensor_scalar(wq_raw[:, k], wq_raw[:, k], cols[:, 3, k:k + 1], SCALE, ALU.mult, ALU.mult)
                V.tensor_scalar(w1_in[:, k], w1_in[:, k], cols[:, 5, k:k + 1], None, ALU.mult)
            V.tensor_scalar(w2_in, w2_in, 0.5, None, ALU.mult).then_inc(dve_setup, 1)
            for dst, src in zip(chunks(wk_hi, permuted), chunks(wqkvo_in[:, 1], raw)):
                V.tensor_copy(dst, src)
            V.tensor_copy(wv_hi[:], wqkvo_in[:, 2])
            V.tensor_copy(wo_hi[:], wqkvo_in[:, 3]).then_inc(dve_setup, 1)
            dve.wait_ge(dve_setup, 3)
            V.tensor_copy(wq_hi[:], wq_raw[:])
            V.tensor_copy(w1_hi[:], w1_in)
            V.tensor_copy(w2_hi[:], w2_in).then_inc(dve_setup, 1)
            for dst, src, hi in zip(chunks(wk_lo, permuted), chunks(wqkvo_in[:, 1], raw), chunks(wk_hi, permuted)):
                V.tensor_tensor(dst, src, hi.bitcast(F32), ALU.subtract)
            V.tensor_tensor(wv_lo[:], wqkvo_in[:, 2], wv_hi[:].bitcast(F32), ALU.subtract)
            V.tensor_tensor(wo_lo[:], wqkvo_in[:, 3], wo_hi[:].bitcast(F32), ALU.subtract)
            dve.wait_ge(dve_setup, 4)
            V.tensor_tensor(wq_lo[:], wq_raw[:], wq_hi[:].bitcast(F32), ALU.subtract)
            V.tensor_tensor(w1_lo[:], w1_in, w1_hi[:].bitcast(F32), ALU.subtract)
            V.tensor_tensor(w2_lo[:], w2_in, w2_hi[:].bitcast(F32), ALU.subtract)
            dve.wait_ge(pe_setup, 4)
            V.tensor_tensor(bq_sum[:], X[:, 0, 0:KD], cols[:, 0], ALU.add)
            V.tensor_tensor(b1_row, S[0:1, 0:FF // BANK].rearrange("p n f -> p (n f)"), rows[:, 4 * D:], ALU.add)
            V.tensor_copy(bo_all[:], X[:, 1, 0:D])
            V.tensor_copy(b2_all[:], X[:, 2, 0:D])
            V.tensor_copy(gamma_all[:], X[:, 2, D:2 * D])
            V.tensor_copy(beta_all[:], X[:, 3, 0:D]).then_inc(dve_setup, 1)
            dve.wait_ge(dve_setup, 5)
            V.tensor_scalar(bq_col[:], bq_sum[:], SCALE, None, ALU.mult)
            V.tensor_copy(b1_stat[0:1], b1_row).then_inc(dve_setup, 1)
            dve.wait_ge(dve_setup, 6)
            V.tensor_tensor(b1_stat[32:33], b1_row, b1_stat[0:1].bitcast(F32), ALU.subtract).then_inc(dve_setup, 1)

            def norm_stats(i, src, stat_sem, mv_sem, b):
                for t in range(QT):
                    last = V.bn_stats(stats[:, i, t], src[:, t])
                last.then_inc(stat_sem, 1)
                dve.wait_ge(stat_sem, done(b))
                settled(dve)
                for t in range(QT):
                    last = V.bn_aggr(mv[:, i, t], stats[:, i, t])
                last.then_inc(mv_sem, 1)

            def norm_apply(i, dst, src):
                for t in range(QT):
                    last = V.tensor_scalar(dst[:, t], src[:, t], mv[:, i, t, 0:1], rstd[:, i, t:t + 1],
                                           ALU.subtract, ALU.mult)
                return last

            def lo_part(dst, src, hi):
                return V.tensor_tensor(dst, src, hi.bitcast(F32), ALU.subtract)

            def bank(b):
                return X[:, b].rearrange("p (k q) -> p k q", k=KD)

            def flat(tile):
                return tile.rearrange("p t e -> p (t e)")

            def x_norm_stats(f):
                dve.wait_ge(x_loaded[f.slot], 16 * (f.half + 1))
                wait(dve, rstd1, number(f))
                norm_stats(0, xs[:, f.slot], stat1, mv1, f)

            def maxima(a, t, half):
                dve.wait_ge(s_ps, done(a, QT, t + 1))
                if t == 0:
                    wait(dve, max_split, number(a))
                banks = slice(2 * half, 2 * half + 2)
                V.tensor_reduce(neg_max[:, t].rearrange("p (b h) -> p b h", b=4)[:, banks],
                                S[:, banks, 0:4 * LK].rearrange("p b (h k) -> p b h k", h=4),
                                axis=AX.X, op=ALU.max, negate=True).then_inc(max_set, 1)

            def hidden(d, u):
                dve.wait_ge(th_set, done(d, NU, u + 1))
                wait(dve, a_split, NU * number(d))
                V.scalar_tensor_tensor(out=act_f[:, u], in0=th[:, u % 2], scalar=1.0, in1=X[:, 2 + u % 2],
                                       op0=ALU.add, op1=ALU.mult).then_inc(act_set, 1)

            def residual_out(e):
                dve.wait_ge(la_ps, done(e, QT))
                V.tensor_scalar(z_den[:], S[:, 2:4, D], Z_EPS, None, ALU.add).then_inc(z_set, 1)
                dve.wait_ge(z_set, done(e))
                V.reciprocal(z_inv[:], z_den[:]).then_inc(z_inved, 1)
                dve.wait_ge(z_inved, done(e))
                wait(dve, y_set, number(e))
                for t in range(QT):
                    last = V.scalar_tensor_tensor(out=x3[:, t], in0=S[:, 2 + t, 0:D], scalar=z_inv[:, t:t + 1],
                                                  in1=x2[:, t], op0=ALU.mult, op1=ALU.add)
                last.then_inc(x3_set, 1)

            def period(dve, f, a, d, e):
                if e is not None:
                    residual_out(e)
                if d is not None:
                    dve.wait_ge(cnT_hid, done(d))
                    lo_part(cnT_lo[:], bank(0), cnT_hi[:]).then_inc(cnT_split, 1)
                if a is not None:
                    dve.wait_ge(kv_hid, done(a, KD))
                    for c in range(KD):
                        lo_part(kv_lo[:, a.slot, c], X[:, 1 + c, 0:KVW], kv_hi[:, a.slot, c]).then_inc(kv_split, 1)
                if f is not None and d is None:
                    dve.wait_ge(cT_hid, done(f))
                    lo_part(cT_lo[:], X[:, 3, 0:KD * LK].rearrange("p (k q) -> p k q", k=KD), cT_hi[:]).then_inc(cT_split, 1)
                if d is not None:
                    dve.wait_ge(wo_ps, done(d))
                    dve.wait_ge(x_bo_set, done(d))
                    V.tensor_tensor(x1[:], bank(0), x_bo[:], ALU.add).then_inc(x1_set, 1)
                    if f is not None:
                        dve.wait_ge(cT_hid, done(f))
                        lo_part(cT_lo[:], X[:, 3, 0:KD * LK].rearrange("p (k q) -> p k q", k=KD), cT_hi[:]
                                ).then_inc(cT_split, 1)
                    dve.wait_ge(x1_set, done(d))
                    norm_stats(1, x1, stat2, mv2, d)
                if f is not None:
                    x_norm_stats(f)
                if e is not None:
                    dve.wait_ge(x3_set, done(e))
                    wait(dve, rstd3, number(e))
                    norm_stats(2, x3, stat3, mv3, e)
                if d is not None:
                    dve.wait_ge(rstd2, done(d))
                    wait(dve, hT_ps, number(d))
                    norm_apply(1, hn, x1).then_inc(hn_set, 1)
                if f is not None:
                    dve.wait_ge(k_hid, done(f, KD))
                    for g in range(KD):
                        last = V.scalar_tensor_tensor(out=k_lo[:, g], in0=X[:, 1, g * LK:(g + 1) * LK],
                                                      scalar=cols[:, 1, g:g + 1], in1=k_hi[:, g].bitcast(F32), op0=ALU.add,
                                                      op1=ALU.subtract)
                    last.then_inc(k_split, 1)
                    dve.wait_ge(rstd1, done(f))
                    wait(dve, xT_ps, number(f))
                    norm_apply(0, xn, xs[:, f.slot]).then_inc(xn_set, 1)
                if d is not None:
                    dve.wait_ge(hT_hid, done(d))
                    lo_part(hT_lo[:], bank(0), hT_hi[:]).then_inc(hT_split, 1)
                if a is not None:
                    maxima(a, 0, 0)
                    maxima(a, 0, 1)
                if d is not None:
                    hidden(d, 0)
                if f is not None:
                    dve.wait_ge(xT_hid, done(f))
                    lo_part(xT_lo[:], bank(1), xT_hi[:]).then_inc(xT_split, 1)
                if d is not None:
                    hidden(d, 1)
                if a is not None:
                    maxima(a, 1, 0)
                if d is not None:
                    hidden(d, 2)
                if a is not None:
                    maxima(a, 1, 1)
                if d is not None:
                    hidden(d, 3)
                if a is not None:
                    dve.wait_ge(max_set, done(a, 2 * QT))
                    wait(dve, maxT_ps, number(a))
                    part = max_parts[:].rearrange("p t (a l m) -> p l t m a", a=2, l=2)
                    neg = neg_max[:].rearrange("p t (m a) -> p t m a", a=2)
                    for t in range(QT):
                        last = V.tensor_copy(part[:, 0, t], neg[:, t])
                    last.then_inc(max_hid, 1)
                    dve.wait_ge(max_hid, done(a))
                    for t in range(QT):
                        last = lo_part(part[:, 1, t], neg[:, t], part[:, 0, t])
                    last.then_inc(max_split, 1)
                if f is not None:
                    dve.wait_ge(c_exped, done(f))
                    wait(dve, kp_split, number(f))
                    V.scalar_tensor_tensor(out=k_phi[:], in0=c_exp[:], scalar=-1.0, in1=cs[:, f.slot], op0=ALU.add,
                                           op1=ALU.max).then_inc(k_phi_set, 1)
                    dve.wait_ge(q_hid, done(f, KD))
                    for g in range(KD):
                        last = V.scalar_tensor_tensor(out=q_lo[:, g], in0=X[:, 0, g * LQ:(g + 1) * LQ],
                                                      scalar=bq_col[:, g:g + 1], in1=q_hi[:, g].bitcast(F32), op0=ALU.add,
                                                      op1=ALU.subtract)
                    last.then_inc(q_split, 1)
                    dve.wait_ge(k_phi_set, done(f))
                    wait(dve, kv_ps, KD * number(f))
                    V.tensor_copy(kp_hi[:], k_phi[:]).then_inc(kp_hid, 1)
                if a is not None:
                    dve.wait_ge(maxT_ps, done(a))
                    wait(dve, max_stacked, 16 * number(a))
                    V.tensor_copy(max_T[:], X[0:4 * PAIRS, 1, 0:LQ]).then_inc(maxT_set, 1)
                if f is not None:
                    dve.wait_ge(kp_hid, done(f))
                    lo_part(kp_lo[:], k_phi[:], kp_hi[:]).then_inc(kp_split, 1)
                if d is not None:
                    dve.wait_ge(f2_ps, done(d))
                    dve.wait_ge(x1_b2_set, done(d))
                    V.tensor_tensor(x2, bank(0), x1_b2[:], ALU.add).then_inc(x2_set, 1)
                    dve.wait_ge(x2_set, done(d))
                    wait(dve, x2_exped, number(d))
                    V.tensor_scalar(x2_min, x2, 0.0, None, ALU.min).then_inc(x2_mined, 1)
                    dve.wait_ge(x2_exped, done(d))
                    wait(dve, qpT_ps, number(d))
                    V.scalar_tensor_tensor(out=flat(q_phi), in0=flat(x2_exp), scalar=-1.0, in1=flat(x2), op0=ALU.add,
                                           op1=ALU.max).then_inc(q_phi_set, 1)
                    dve.wait_ge(qpT_hid, done(d))
                    lo_part(qpT_lo[:], bank(1), qpT_hi[:]).then_inc(qpT_split, 1)
                if a is not None:
                    dve.wait_ge(aug_ps, done(a))
                    heads = S[:, 0:QT].rearrange("p t (h w) -> p t h w", w=VW)
                    V.reciprocal(den_inv[:], heads[:, :, :, DH]).then_inc(den_set, 1)
                    dve.wait_ge(den_set, done(a))
                    wait(dve, cnT_ps, number(a))
                    for t in range(QT):
                        for g in range(KD):
                            val = heads[:, t, :, 0:DH].rearrange("p (j g a) e -> p g j a e", g=KD, a=2)[:, g]
                            inv = den_inv[:, t].rearrange("p (j g a) -> p g j a", g=KD, a=2)[:, g]
                            last = V.tensor_tensor(cn[:, t, g * P:(g + 1) * P].rearrange("p (j a e) -> p j a e", a=2, e=DH),
                                                   val, inv[:, :, :, None].to_broadcast([P, H // 4, 2, DH]), ALU.mult)
                    last.then_inc(cn_set, 1)

            periods(dve, period)

        @block.gpsimd
        def _(pool):
            G = nc.gpsimd
            G.memset(ident[:], 0.0).then_inc(ident_set, 1)
            pool.wait_ge(ident_set, 1)
            G.affine_select(out=ident[:], in_=ident[:], compare_op=ALU.not_equal, fill=1.0, base=0,
                            pattern=[[-1, P]], channel_multiplier=1).then_inc(ident_set, 1)
            pool.wait_ge(dve_setup, SETUP_STEPS)
            pool.wait_ge(dve_consts, 4)

            def inverse_deviation(i, mv_sem, var_sem, rstd_sem, b):
                pool.wait_ge(mv_sem, done(b))
                settled(pool)
                G.tensor_scalar(var_eps[:, i], mv[:, i, :, 1], 1.0, LN_EPS, ALU.mult, ALU.add).then_inc(var_sem, 1)
                pool.wait_ge(var_sem, done(b))
                G.tensor_tensor(rstd[:, i], var_eps[:, i], minus_half[:], ALU.pow).then_inc(rstd_sem, 1)

            def finish(d):
                inverse_deviation(2, mv3, var3, rstd3, d)
                pool.wait_ge(rstd3, done(d))
                G.tensor_tensor(mean_rstd[:], mv[:, 2, :, 0], rstd[:, 2], ALU.mult).then_inc(mean_set, 1)
                pool.wait_ge(mean_set, done(d))
                settled(pool)
                G.tensor_scalar(mean_shift[:], mean_rstd[:], -1.0, 0.0, ALU.mult, ALU.add).then_inc(shift_set, 1)
                pool.wait_ge(shift_set, done(d))
                settled(pool)
                for t in range(QT):
                    last = G.tensor_scalar(y[:, t], x3[:, t], rstd[:, 2, t:t + 1], mean_shift[:, t:t + 1],
                                           ALU.mult, ALU.add)
                last.then_inc(y_set, 1)
                pool.wait_ge(y_set, done(d))
                for t in range(QT):
                    last = G.tensor_tensor(yg[:, t], y[:, t], gamma_all[:], ALU.mult)
                last.then_inc(yg_set, 1)
                pool.wait_ge(yg_set, done(d))
                wait(pool, stored, 16 * number(d))
                for t in range(QT):
                    last = G.tensor_tensor(y_out[:, t], yg[:, t], beta_all[:], ALU.add)
                last.then_inc(y_out_set, 1)

            def period(pool, f, a, d, e):
                if f is not None:
                    pool.wait_ge(c_loaded[f.slot], 16 * (f.half + 1))
                    wait(pool, kv_ps, KD * number(f))
                    settled(pool)
                    G.tensor_scalar(c_hi[:, 0:D], cs[:, f.slot], 1.0, 0.0, ALU.mult, ALU.add).then_inc(c_hid, 1)
                    pool.wait_ge(c_hid, done(f))
                    G.tensor_tensor(c_lo[:, 0:D], cs[:, f.slot], c_hi[:, 0:D].bitcast(F32), ALU.subtract).then_inc(c_split, 1)
                if d is not None:
                    inverse_deviation(1, mv2, var2, rstd2, d)
                if f is not None:
                    inverse_deviation(0, mv1, var1, rstd1, f)
                if d is not None:
                    pool.wait_ge(x1_set, done(d))
                    wait(pool, x2_set, number(d))
                    for t in range(QT):
                        last = G.tensor_tensor(x1_b2[:, t], x1[:, t], b2_all[:], ALU.add)
                    last.then_inc(x1_b2_set, 1)
                    for u in range(NU):
                        pool.wait_ge(a_hid, done(d, NU, u + 1))
                        if u == 0:
                            wait(pool, f2_ps, number(d))
                        G.tensor_tensor(a_lo[:, u], act_f[:, u], a_hi[:, u].bitcast(F32), ALU.subtract).then_inc(a_split, 1)
                if a is not None:
                    pool.wait_ge(x_loaded[a.slot], 16 * (a.half + 1))
                    wait(pool, x1_set, number(a))
                    for t in range(QT):
                        last = G.tensor_tensor(x_bo[:, t], xs[:, a.slot, t], bo_all[:], ALU.add)
                    last.then_inc(x_bo_set, 1)
                if e is not None:
                    finish(e)

            periods(pool, period)


_INS = ['x', 'ctx_1024', 'L0_xattn_Wq', 'L0_xattn_bq', 'L0_xattn_Wk', 'L0_xattn_bk', 'L0_xattn_Wv', 'L0_xattn_bv',
        'L0_xattn_Wo', 'L0_xattn_bo', 'L0_xattn_W1', 'L0_xattn_b1', 'L0_xattn_W2', 'L0_xattn_b2', 'L0_xattn_ln_q_g',
        'L0_xattn_ln_q_b', 'L0_xattn_ln_ff_g', 'L0_xattn_ln_ff_b', 'L1_xattn_gamma', 'L1_xattn_beta']


def kernel(**inputs):
    import numpy as _np
    import concourse.bacc as _bacc
    from concourse import mybir as _mybir
    from concourse.bass_utils import run_bass_kernel_spmd as _run

    nc = _bacc.Bacc("TRN2", target_bir_lowering=False, num_devices=1)
    arrays, args = {}, []
    for name in _INS:
        a = _np.ascontiguousarray(inputs[name])
        arrays[f"in_{name}_dram"] = a
        args.append(nc.dram_tensor(f"in_{name}_dram", a.shape, _mybir.dt.from_np(a.dtype), kind="ExternalInput").ap())
    args.append(nc.dram_tensor("out_0_dram", inputs["x"].shape, _mybir.dt.float32, kind="ExternalOutput").ap())
    build(nc, *args)
    r = _run(nc, [arrays], core_ids=[0])
    return r.results[0]["out_0_dram"]
```

```python
from collections import namedtuple
from contextlib import ExitStack

import concourse.bass as bass
from concourse import mybir

F32 = mybir.dt.float32
F32R = mybir.dt.float32r
ALU = mybir.AluOpType
ACT = mybir.ActivationFunctionType
AX = mybir.AxisListType

Batch = namedtuple("Batch", "half slot")


def number(b):
    return 2 * b.half + b.slot


def done(b, per=1, k=None):
    return per * number(b) + (per if k is None else k)


def wait(eng, sem, count):
    if not isinstance(count, int) or count > 0:
        eng.wait_ge(sem, count)


def build(nc, x, ctx, Wq, bq, Wk, bk, Wv, bv, Wo, bo, W1, b1, W2, b2,
          ln_q_g, ln_q_b, ln_ff_g, ln_ff_b, gamma, beta, out):
    P = 128
    B, LQ, D = x.shape
    LK = ctx.shape[1]
    FF = W1.shape[1]
    H = 16
    DH = D // H
    QT = LQ // P
    KD = D // P
    PAIRS = H // 2
    NU = FF // (2 * P)
    BANK = 512
    VW = 32
    KVW = D + 2
    PARTS = 3
    LN_EPS = 1e-5
    Z_EPS = 1e-6
    SCALE = float(DH) ** -0.5
    assert QT == 2 and KD == 2 and B % 2 == 0 and B >= 10 and QT * D == BANK and SCALE == 0.25

    es = ExitStack()
    with es:
        def sb(name, shape, dt=F32):
            return es.enter_context(nc.sbuf_tensor(name, shape, dt))

        def sem(name):
            return es.enter_context(nc.semaphore(name))

        wq_hi, wq_lo = sb("wq_hi", [P, KD, D], F32R), sb("wq_lo", [P, KD, D], F32R)
        wkv_hi, wkv_lo = sb("wkv_hi", [P, KD, 2 * D], F32R), sb("wkv_lo", [P, KD, 2 * D], F32R)
        wo_hi, wo_lo = sb("wo_hi", [P, KD, D], F32R), sb("wo_lo", [P, KD, D], F32R)
        w1_hi, w1_lo = sb("w1_hi", [P, KD, FF], F32R), sb("w1_lo", [P, KD, FF], F32R)
        w2_hi, w2_lo = sb("w2_hi", [P, FF // P, D], F32R), sb("w2_lo", [P, FF // P, D], F32R)
        cols = sb("cols", [P, 7, KD])
        bq_sum, bq_col, q_gain = sb("bq_sum", [P, KD]), sb("bq_col", [P, KD]), sb("q_gain", [P, KD])
        b1_raw, b1_col, b1_half = (sb(n, [P, FF // P]) for n in ("b1_raw", "b1_col", "b1_half"))
        ones = sb("ones", [P, LQ])
        bv_wide = sb("bv_wide", [P, KD, P])
        bo_all, b2_all = sb("bo_all", [P, D]), sb("b2_all", [P, D])
        gamma_all, beta_all = sb("gamma_all", [P, D]), sb("beta_all", [P, D])
        ident = sb("ident", [P, P])
        minus_half = sb("minus_half", [P, QT])

        xs = sb("xs", [P, 2, QT, D])
        cs = sb("cs", [LK, 2, D])
        x_bo = sb("x_bo", [P, QT, D])
        stats = sb("stats", [P, 3, QT, 6])
        mv = sb("mv", [P, 3, QT, 2])
        var_eps = sb("var_eps", [P, 3, QT])
        rstd = sb("rstd", [P, 3, QT])
        xn = sb("xn", [P, QT, D])
        xT_hi, xT_lo = sb("xT_hi", [P, KD, LQ], F32R), sb("xT_lo", [P, KD, LQ], F32R)
        cT_hi, cT_lo = sb("cT_hi", [P, KD, LK], F32R), sb("cT_lo", [P, KD, LK], F32R)
        q_hi, q_lo = sb("q_hi", [P, KD, LQ], F32R), sb("q_lo", [P, KD, LQ], F32R)
        k_rows = sb("k_rows", [LK, D])
        k_hi, k_lo = sb("k_hi", [P, KD, LK], F32R), sb("k_lo", [P, KD, LK], F32R)
        q_stack = sb("q_stack", [P, PAIRS, LQ], F32R)
        k_stack = sb("k_stack", [P, 2, PAIRS, LK], F32R)
        v_aug = sb("v_aug", [LK, 2, H, VW])
        neg_max = sb("neg_max", [P, QT, H])
        max_parts = sb("max_parts", [P, QT, 4 * PAIRS], F32R)
        max_T = sb("max_T", [4 * PAIRS, LQ], F32R)
        probs = sb("probs", [LK, H, LQ])
        aug = sb("aug", [P, H // 4, LQ])
        den_inv = sb("den_inv", [P, QT, H])
        cn = sb("cn", [P, QT, D])
        cnT_hi, cnT_lo = sb("cnT_hi", [P, KD, LQ], F32R), sb("cnT_lo", [P, KD, LQ], F32R)
        c_min, c_exp, k_phi = sb("c_min", [LK, D]), sb("c_exp", [LK, D]), sb("k_phi", [LK, D])
        c_hi, c_lo = sb("c_hi", [LK, KVW], F32R), sb("c_lo", [LK, KVW], F32R)
        kp_hi, kp_lo = sb("kp_hi", [LK, D], F32R), sb("kp_lo", [LK, D], F32R)
        kv_hi, kv_lo = sb("kv_hi", [P, 2, KD, KVW], F32R), sb("kv_lo", [P, 2, KD, KVW], F32R)
        x1, hn = sb("x1", [P, QT, D]), sb("hn", [P, QT, D])
        x1_b2 = sb("x1_b2", [P, 2, QT, D])
        hT_hi, hT_lo = sb("hT_hi", [P, KD, LQ], F32R), sb("hT_lo", [P, KD, LQ], F32R)
        th, hid = sb("th", [P, 2, BANK]), sb("hid", [P, 2, BANK])
        act_f = sb("act_f", [P, NU, BANK])
        a_hi, a_lo = sb("a_hi", [P, NU, BANK], F32R), sb("a_lo", [P, NU, BANK], F32R)
        x2_tiles = sb("x2_tiles", [P, 4, QT, D])
        x2, x2_min, x2_exp, q_phi = (x2_tiles[:, i] for i in range(4))
        qpT_hi, qpT_lo = sb("qpT_hi", [P, KD, LQ], F32R), sb("qpT_lo", [P, KD, LQ], F32R)
        z_den, z_inv = sb("z_den", [P, QT]), sb("z_inv", [P, QT])
        x3_tiles = sb("x3_tiles", [P, 4, QT, D])
        x3, y, yg, y_out = (x3_tiles[:, i] for i in range(4))
        mean_rstd, mean_shift = sb("mean_rstd", [P, QT]), sb("mean_shift", [P, QT])

        wq_raw = hn
        rows = probs[0:1].rearrange("o h q -> o (h q)")[:, 0:4 * D]
        w1_in = act_f[:].rearrange("p u (i n) -> p (u i n)", i=2).rearrange("p (k n) -> p k n", k=KD)
        w2_in = x2_tiles[:].rearrange("p i t e -> p (i t e)").rearrange("p (c n) -> p c n", n=D)
        wqkvo_in = x3_tiles[:].rearrange("p i t e -> p (i t e)").rearrange("p (i k n) -> p i k n", i=4, k=KD)

        S = es.enter_context(nc.psum_tensor("S", [P, 4, BANK], F32))
        X = es.enter_context(nc.psum_tensor("X", [P, 4, BANK], F32))

        wq_loaded, wkv_loaded, small_loaded, w2_loaded, dense_small_loaded = (
            sem(n) for n in ("wq_loaded", "wkv_loaded", "small_loaded", "w2_loaded", "dense_small_loaded"))
        gain_loaded, wo_w1_loaded = sem("gain_loaded"), sem("wo_w1_loaded")
        passed, ones_set, wq_ordered, fixed_set, ident_set = (
            sem(n) for n in ("passed", "ones_set", "wq_ordered", "fixed_set", "ident_set"))
        k_fixed = sem("k_fixed")
        bq_ps, b1_ps, rows_ps, w_hid, dense_hid, gain_set, bq_set, proj_set = (
            sem(n) for n in ("bq_ps", "b1_ps", "rows_ps", "w_hid", "dense_hid", "gain_set", "bq_set", "proj_set"))
        bv_spread, b1_set, dense_set = (sem(n) for n in ("bv_spread", "b1_set", "dense_set"))
        x_loaded = [sem(f"x_loaded{i}") for i in range(2)]
        c_loaded = [sem(f"c_loaded{i}") for i in range(2)]
        q_stacked, k_stacked, max_stacked, stored = (sem(n) for n in ("q_stacked", "k_stacked", "max_stacked", "stored"))
        xT_ps, cT_ps, q_ps, k_ps, kv_rows_ps, kv_ps, s_ps, maxT_ps, st_ps, pv_ps, aug_ps = (
            sem(n) for n in ("xT_ps", "cT_ps", "q_ps", "k_ps", "kv_rows_ps", "kv_ps", "s_ps", "maxT_ps", "st_ps", "pv_ps",
                             "aug_ps"))
        cnT_ps, wo_ps, hT_ps, f1_ps, f2_ps, qpT_ps, la_ps = (
            sem(n) for n in ("cnT_ps", "wo_ps", "hT_ps", "f1_ps", "f2_ps", "qpT_ps", "la_ps"))
        xT_hid, cT_hid, q_hid, k_hid, k_copied, v_copied, c_exped, kv_hid, probs_set, aug_set = (
            sem(n) for n in ("xT_hid", "cT_hid", "q_hid", "k_hid", "k_copied", "v_copied", "c_exped", "kv_hid", "probs_set",
                             "aug_set"))
        cnT_hid, hT_hid, hid_set, a_hid, x2_exped, qpT_hid = (
            sem(n) for n in ("cnT_hid", "hT_hid", "hid_set", "a_hid", "x2_exped", "qpT_hid"))
        stat1, mv1, xn_set, xT_split, cT_split, q_split, k_split, k_phi_set, kp_hid, kp_split, kv_split = (
            sem(n) for n in ("stat1", "mv1", "xn_set", "xT_split", "cT_split", "q_split", "k_split", "k_phi_set", "kp_hid",
                             "kp_split", "kv_split"))
        max_set, max_hid, max_split, maxT_set, den_set, cn_set, cnT_split = (
            sem(n) for n in ("max_set", "max_hid", "max_split", "maxT_set", "den_set", "cn_set", "cnT_split"))
        x1_set, stat2, mv2, hn_set, hT_split, act23_set, x2_set, q_phi_set, qpT_split, z_set, z_inved, x3_set, stat3, mv3 = (
            sem(n) for n in ("x1_set", "stat2", "mv2", "hn_set", "hT_split", "act23_set", "x2_set", "q_phi_set", "qpT_split",
                             "z_set", "z_inved", "x3_set", "stat3", "mv3"))
        c_mined, c_hid, c_split, x_bo_set, var1, rstd1, var2, rstd2, x1_b2_set, a_split, x2_mined, var3, rstd3 = (
            sem(n) for n in ("c_mined", "c_hid", "c_split", "x_bo_set", "var1", "rstd1", "var2", "rstd2", "x1_b2_set",
                             "a_split", "x2_mined", "var3", "rstd3"))
        plus_set, act01_set = sem("plus_set"), sem("act01_set")
        mean_set, shift_set, y_set, yg_set, y_out_set = (sem(n) for n in ("mean_set", "shift_set", "y_set", "yg_set", "y_out_set"))

        SMALL_COUNT, DENSE_SMALL_COUNT, FIXED_COUNT = 16 * 5, 16 * 8, 4

        block = es.enter_context(nc.Block())

        def periods(eng, period, set_up_projections=None):
            def line(n):
                return [Batch(m // 2, m % 2) if 0 <= m < B else None for m in (n + 1, n, n - 1, n - 2, n - 3, n - 4)]

            for n in range(-1, 6):
                period(eng, *line(n))
                if n == -1 and set_up_projections is not None:
                    set_up_projections()
            with eng.Fori(0, B // 2 - 4) as j:
                period(eng, Batch(j + 3, 1), Batch(j + 3, 0), Batch(j + 2, 1), Batch(j + 2, 0), Batch(j + 1, 1), Batch(j + 1, 0))
                period(eng, Batch(j + 4, 0), Batch(j + 3, 1), Batch(j + 3, 0), Batch(j + 2, 1), Batch(j + 2, 0), Batch(j + 1, 1))
            for n in range(B - 2, B + 4):
                period(eng, *line(n))

        raw, permuted = "p (g j r) -> p g r j", "p (g r j) -> p g r j"

        def chunks(w, order):
            return [w[:, k, 0:D].rearrange(order, g=KD, r=2 * DH) for k in range(KD)]

        def settled(eng):
            eng.sem_inc(passed)

        def is_first(b):
            return isinstance(b.half, int) and b == Batch(0, 0)

        @block.sync
        def _(sp):
            def load_x(b):
                wait(sp, x_bo_set, number(b) - 1)
                sp.dma_start(xs[:, b.slot], x[bass.ds(number(b), 1)].rearrange("b (t p) d -> p (b t) d", p=P)
                             ).then_inc(x_loaded[b.slot], 16)

            def load_c(b):
                for sem_ in (cT_ps, k_phi_set, c_split):
                    wait(sp, sem_, number(b) - 1)
                sp.dma_start(cs[:, b.slot], ctx[bass.ds(number(b), 1)].rearrange("b k d -> k (b d)")
                             ).then_inc(c_loaded[b.slot], 16)

            def load_weight(dst, w, sem_):
                sp.dma_start(dst, w.rearrange("(k p) n -> p k n", p=P)).then_inc(sem_, 16)

            def load_columns(i, v, sem_):
                sp.dma_start(cols[:, i], v.rearrange("(k p) -> p k", p=P), allow_slow_non_contiguous=True).then_inc(sem_, 16)

            load_weight(wqkvo_in[:, 0], Wq, wq_loaded)
            load_x(Batch(0, 0))
            load_c(Batch(0, 0))
            load_columns(3, ln_q_g, gain_loaded)
            load_columns(4, ln_q_b, small_loaded)
            load_weight(wqkvo_in[:, 1], Wk, wkv_loaded)
            load_weight(wqkvo_in[:, 2], Wv, wkv_loaded)
            for i, v in enumerate((bq, bk)):
                for g in range(KD):
                    sp.dma_start(cols[:, i, g:g + 1], v[g * P:(g + 1) * P].rearrange("(j r o) -> r j o", r=2 * DH, o=1),
                                 allow_slow_non_contiguous=True).then_inc(small_loaded, 16)
            load_x(Batch(0, 1))
            load_c(Batch(0, 1))
            load_weight(wqkvo_in[:, 3], Wo, wo_w1_loaded)
            load_weight(w1_in, W1, wo_w1_loaded)
            for i, v in ((2, bv), (5, ln_ff_g), (6, ln_ff_b)):
                load_columns(i, v, dense_small_loaded)
            sp.dma_start(b1_raw[:], b1.rearrange("(k p) -> p k", p=P), allow_slow_non_contiguous=True
                         ).then_inc(dense_small_loaded, 16)
            for i, v in enumerate((bo, b2, gamma, beta)):
                sp.dma_start(rows[:, i * D:(i + 1) * D], v.rearrange("(a d) -> a d", a=1)).then_inc(dense_small_loaded, 16)
            load_weight(w2_in, W2, w2_loaded)

            def store(d):
                sp.wait_ge(y_out_set, done(d))
                sp.dma_start(out[bass.ds(number(d), 1)].rearrange("b (t p) d -> p (b t) d", p=P), y_out
                             ).then_inc(stored, 16)

            def period(sp, g, f, a, b, d, e):
                new = g is not None and not (isinstance(g.half, int) and g.half == 0)
                if a is not None:
                    sp.wait_ge(maxT_set, done(a))
                    sp.dma_start(q_stack[96:100].bitcast(F32), max_T[:].bitcast(F32)).then_inc(max_stacked, 16)
                if new:
                    load_x(g)
                    load_c(g)
                if f is not None:
                    if is_first(f):
                        sp.wait_ge(k_fixed, 3)
                    if a is not None:
                        sp.wait_ge(st_ps, done(a, PAIRS))
                        settled(sp)
                    sp.wait_ge(k_split, done(f))
                    settled(sp)
                    for part, src in enumerate((k_hi, k_lo, k_hi)):
                        for ab in range(2):
                            r = 32 * part + DH * ab
                            sp.dma_start(k_stack[r:r + DH, ab].bitcast(F32), src[64 * ab:64 * ab + 64].bitcast(F32)
                                         ).then_inc(k_stacked, 16)
                    sp.wait_ge(q_split, done(f))
                    for part, src in enumerate((q_hi, q_hi, q_lo)):
                        sp.dma_start(q_stack[32 * part:32 * part + 32].bitcast(F32), src[:].bitcast(F32)
                                     ).then_inc(q_stacked, 16)
                if e is not None:
                    store(e)

            periods(sp, period)
            sp.wait_ge(stored, 16 * B)

        K_DMAS, Q_DMAS = PARTS * 2, PARTS

        @block.tensor
        def _(pe):
            def split_mm(out_, stat, mov, n):
                parts = [(c, s, m) for c in range(n) for s, m in ((0, 1), (1, 0), (0, 0))]
                for i, (c, s, m) in enumerate(parts):
                    last = nc.tensor.matmul(out_, stat(c, s), mov(c, m), start=(i == 0), stop=(i == len(parts) - 1))
                return last

            pe.wait_ge(ident_set, 2)

            def query_bias():
                pe.wait_ge(wq_ordered, 1)
                pe.wait_ge(small_loaded, SMALL_COUNT)
                for m in range(KD):
                    for k in range(KD):
                        last = nc.tensor.matmul(S[:, 3, m:m + 1], wq_raw[:, k, m * P:(m + 1) * P], cols[:, 4, k:k + 1],
                                                start=(k == 0), stop=(k == KD - 1))
                last.then_inc(bq_ps, 1)

            def ffn_bias():
                pe.wait_ge(wo_w1_loaded, 16 * 2)
                pe.wait_ge(dense_small_loaded, DENSE_SMALL_COUNT)
                for m in range(FF // P):
                    for k in range(KD):
                        last = nc.tensor.matmul(S[:, 0, m:m + 1], w1_in[:, k, m * P:(m + 1) * P], cols[:, 6, k:k + 1],
                                                start=(k == 0), stop=(k == KD - 1))
                last.then_inc(b1_ps, 1)

            def spread_rows():
                pe.wait_ge(bv_spread, 1)
                for k in range(KD):
                    nc.tensor.matmul(S[:, 2, 0:D], bv_wide[:, k], wqkvo_in[:, 3, k], start=(k == 0), stop=False)
                nc.tensor.matmul(S[:, 2, 0:D], ones[0:1, 0:P], rows[:, 0:D], start=False, stop=True)
                for i, o in ((1, S[:, 2, D:2 * D]), (2, S[:, 3, 0:D]), (3, S[:, 3, D:2 * D])):
                    last = nc.tensor.matmul(o, ones[0:1, 0:P], rows[:, i * D:(i + 1) * D], start=True, stop=True)
                last.then_inc(rows_ps, 1)

            def rows_to_columns(out_, src):
                for k in range(KD):
                    for t in range(QT):
                        last = nc.tensor.transpose(out_[:, k * LQ + t * P:k * LQ + (t + 1) * P],
                                                   src[:, t, k * P:(k + 1) * P], ident[:])
                return last


            def context_columns(f, a, d, e):
                pe.wait_ge(c_loaded[f.slot], 16 * (f.half + 1))
                if e is not None:
                    pe.wait_ge(x2_set, done(e))
                elif d is not None:
                    pe.wait_ge(x1_set, done(d))
                elif a is not None:
                    pe.wait_ge(cT_split, done(a))
                for k in range(KD):
                    last = nc.tensor.transpose(X[:, 0, k * LK:(k + 1) * LK], cs[:, f.slot, k * P:(k + 1) * P],
                                               ident[0:LK, 0:LK])
                last.then_inc(cT_ps, 1)

            def q_phi_columns(e, a):
                pe.wait_ge(q_phi_set, done(e))
                if a is not None:
                    pe.wait_ge(q_split, done(a))
                rows_to_columns(X[:, 1], q_phi).then_inc(qpT_ps, 1)

            def attention_rows(b):
                pe.wait_ge(aug_set, done(b, 2))
                pe.wait_ge(probs_set, done(b, PAIRS))
                for t in range(QT):
                    for G in range(H // 4):
                        last = nc.tensor.transpose(S[:, t, G * P:(G + 1) * P], aug[:, G, t * P:(t + 1) * P], ident[:])
                last.then_inc(aug_ps, 1)

            def project_kv(f, a, b):
                pe.wait_ge(cT_split, done(f))
                if b is not None:
                    pe.wait_ge(aug_set, done(b, 2))
                elif a is not None:
                    pe.wait_ge(v_copied, done(a))
                split_mm(X[0:LK, 3, 0:2 * D], lambda c, s: (cT_hi, cT_lo)[s][:, c],
                         lambda c, m: (wkv_hi, wkv_lo)[m][:, c], KD).then_inc(kv_rows_ps, 1)

            def linear_attention(e, b):
                pe.wait_ge(qpT_split, done(e))
                pe.wait_ge(kv_split, done(e, KD))
                if b is not None:
                    pe.wait_ge(probs_set, done(b, PAIRS))
                else:
                    pe.wait_ge(x3_set, number(e))
                for t in range(QT):
                    split_mm(S[:, 2 + t, 0:KVW], lambda c, s: (qpT_hi, qpT_lo)[s][:, c, t * P:(t + 1) * P],
                             lambda c, m: (kv_hi, kv_lo)[m][:, e.slot, c], KD).then_inc(la_ps, 1)

            def ffn_up(d, b, f, u, i):
                if u == 0 and i == 0:
                    pe.wait_ge(hT_split, done(d))
                    if b is not None:
                        pe.wait_ge(aug_set, done(b, 2))
                    else:
                        pe.wait_ge(kv_split, done(d, KD))
                if u == 1 and i == 0 and f is not None:
                    pe.wait_ge(v_copied, done(f))
                if u >= 2 and i == 0:
                    pe.wait_ge(hid_set, done(d, NU, u - 1))
                m = 2 * u + i
                o = X[:, 2 + u % 2, i * LQ:(i + 1) * LQ]
                parts = [(c, s, v) for c in range(KD) for s, v in ((0, 1), (1, 0), (0, 0))]
                for n, (c, s, v) in enumerate(parts):
                    last = nc.tensor.matmul(o, (w1_hi, w1_lo)[s][:, c, m * P:(m + 1) * P], (hT_hi, hT_lo)[v][:, c],
                                            start=(n == 0), stop=(n == len(parts) - 1))
                if i == 1:
                    last.then_inc(f1_ps, 1)

            def scores(a, b, e, t, half):
                if t == 0 and half == 0:
                    pe.wait_ge(k_stacked, 16 * K_DMAS * done(a))
                    pe.wait_ge(q_stacked, 16 * Q_DMAS * done(a))
                    if b is not None:
                        pe.wait_ge(cn_set, done(b))
                if t == 0 and half == 1 and e is not None:
                    pe.wait_ge(x3_set, done(e))
                if t > 0:
                    pe.wait_ge(max_set, done(a, 2 * QT, 2 * (t - 1) + half + 1))
                for p in range(half * PAIRS // 2, (half + 1) * PAIRS // 2):
                    last = nc.tensor.matmul(S[:, p // 2, (p % 2) * 2 * LK:(p % 2 + 1) * 2 * LK],
                                            q_stack[0:96, p, t * P:(t + 1) * P],
                                            k_stack[0:96, :, p], start=True, stop=True)
                last.then_inc(s_ps, 1)

            def attention_columns(b, f, d, e):
                pe.wait_ge(cn_set, done(b))
                if f is not None:
                    pe.wait_ge(cT_split, done(f))
                elif e is not None:
                    pe.wait_ge(x2_set, done(e))
                rows_to_columns(X[:, 0], cn).then_inc(cnT_ps, 1)

            def k_columns(f, a, e):
                pe.wait_ge(k_copied, done(f))
                if e is not None:
                    pe.wait_ge(qpT_split, done(e))
                elif a is not None:
                    pe.wait_ge(q_split, done(a))
                for g in range(KD):
                    last = nc.tensor.transpose(X[:, 1, g * LK:(g + 1) * LK], k_rows[:, g * P:(g + 1) * P], ident[0:LK, 0:LK])
                last.then_inc(k_ps, 1)

            def project_o(b):
                pe.wait_ge(cnT_split, done(b))
                for t in range(QT):
                    last = split_mm(X[:, 0, t * D:(t + 1) * D], lambda c, s: (cnT_hi, cnT_lo)[s][:, c, t * P:(t + 1) * P],
                                    lambda c, m: (wo_hi, wo_lo)[m][:, c], KD)
                last.then_inc(wo_ps, 1)

            def max_columns(a):
                pe.wait_ge(max_set, done(a, 2 * QT))
                pe.wait_ge(max_split, done(a))
                for t in range(QT):
                    last = nc.tensor.transpose(S[0:4 * PAIRS, 0, t * P:(t + 1) * P], max_parts[:, t].bitcast(F32), ident[:])
                last.then_inc(maxT_ps, 1)

            def x_columns(f):
                pe.wait_ge(xn_set, done(f))
                pe.wait_ge(k_split, done(f))
                rows_to_columns(X[:, 1], xn).then_inc(xT_ps, 1)

            def project_q(f):
                pe.wait_ge(xT_split, done(f))
                for g in range(KD):
                    last = split_mm(X[:, 1, g * LQ:(g + 1) * LQ],
                                    lambda c, s: (wq_hi, wq_lo)[s][:, c, g * P:(g + 1) * P],
                                    lambda c, m: (xT_hi, xT_lo)[m][:, c], KD)
                last.then_inc(q_ps, 1)

            def hidden_columns(b, a):
                pe.wait_ge(hn_set, done(b))
                if a is not None:
                    pe.wait_ge(max_set, done(a, 2 * QT, 2 * QT - 1))
                rows_to_columns(S[:, 1], hn).then_inc(hT_ps, 1)

            def linear_state(b, d, f):
                pe.wait_ge(kp_split, done(b))
                pe.wait_ge(c_split, done(b))
                if d is not None:
                    pe.wait_ge(hid_set, done(d, NU))
                elif f is not None:
                    pe.wait_ge(v_copied, done(f))
                for c in range(KD):
                    split_mm(X[:, 2 + c, 0:KVW], lambda _, s: (kp_hi, kp_lo)[s][:, c * P:(c + 1) * P],
                             lambda _, m: (c_hi, c_lo)[m][:], 1).then_inc(kv_ps, 1)

            def ffn_down(d, b, e, u, t):
                if (u, t) == (0, 0) and b is not None:
                    pe.wait_ge(x1_set, done(b))
                elif (u, t) == (0, 0) and e is not None:
                    pe.wait_ge(x2_set, done(e))
                if t == 0:
                    pe.wait_ge(a_split, done(d, NU, u + 1))
                for i in range(2):
                    for s, v in ((0, 1), (1, 0), (0, 0)):
                        lo = i * LQ + t * P
                        last = nc.tensor.matmul(X[:, 0, t * D:(t + 1) * D], (a_hi, a_lo)[s][:, u, lo:lo + P],
                                                (w2_hi, w2_lo)[v][:, 2 * u + i],
                                                start=(u == 0 and t == 0 and i == 0 and (s, v) == (0, 1)),
                                                stop=(u == NU - 1 and t == QT - 1 and i == 1 and (s, v) == (0, 0)))
                if u == NU - 1 and t == QT - 1:
                    last.then_inc(f2_ps, 1)

            def scores_T(a, b, p):
                if p == 0:
                    pe.wait_ge(max_stacked, 16 * done(a))
                    pe.wait_ge(maxT_set, done(a))
                    if b is not None:
                        pe.wait_ge(hT_split, done(b))
                if p >= 4:
                    pe.wait_ge(probs_set, done(a, PAIRS, p - 3))
                for ab in range(2):
                    last = nc.tensor.matmul(S[0:LK, p % 4, ab * LQ:(ab + 1) * LQ], k_stack[0:100, ab, p],
                                            q_stack[0:100, p], start=True, stop=True)
                last.then_inc(st_ps, 1)

            def attend(a, b, f, G):
                pe.wait_ge(probs_set, done(a, PAIRS, 2 * G + 2))
                if G == 0:
                    pe.wait_ge(v_copied, done(a))
                    if b is not None:
                        pe.wait_ge(kv_split, done(b, KD))
                    elif f is not None:
                        pe.wait_ge(v_copied, done(f))
                for c in range(4):
                    h = 4 * G + c
                    last = nc.tensor.matmul(X[32 * c:32 * c + VW, 2 + G // 2, (G % 2) * LQ:(G % 2 + 1) * LQ],
                                            v_aug[:, a.slot, h], probs[:, h], start=True, stop=True)
                if G % 2 == 1:
                    last.then_inc(pv_ps, 1)

            def period(pe, g, f, a, b, d, e):
                def up(u, halves=range(2)):
                    if d is not None:
                        for i in halves:
                            ffn_up(d, b, f, u, i)

                def down(u, tiles=range(QT)):
                    if d is not None:
                        for t in tiles:
                            ffn_down(d, b, e, u, t)

                if f is not None:
                    context_columns(f, a, d, e)
                    if is_first(f):
                        query_bias()
                        pe.wait_ge(proj_set, 1)
                if e is not None:
                    q_phi_columns(e, a)
                if b is not None:
                    attention_rows(b)
                if f is not None:
                    project_kv(f, a, b)
                if e is not None:
                    linear_attention(e, b)
                up(0)
                if b is not None:
                    attention_columns(b, f, d, e)
                if f is not None:
                    k_columns(f, a, e)
                up(1, [0])
                if a is not None:
                    if is_first(a):
                        pe.wait_ge(dense_set, 1)
                    scores(a, b, e, 0, 0)
                    scores(a, b, e, 0, 1)
                up(1, [1])
                if b is not None:
                    project_o(b)
                if a is not None:
                    scores(a, b, e, 1, 0)
                    scores(a, b, e, 1, 1)
                up(2)
                if f is not None:
                    x_columns(f)
                    if is_first(f):
                        ffn_bias()
                up(3)
                down(0)
                if a is not None:
                    max_columns(a)
                if f is not None:
                    if is_first(f):
                        pe.wait_ge(bq_set, 2)
                    project_q(f)
                    if is_first(f):
                        spread_rows()
                if b is not None:
                    hidden_columns(b, a)
                down(1)
                if b is not None:
                    linear_state(b, d, f)
                if a is not None:
                    for p in range(4):
                        scores_T(a, b, p)
                down(2)
                if a is not None:
                    scores_T(a, b, 4)
                    scores_T(a, b, 5)
                down(3)
                if a is not None:
                    scores_T(a, b, 6)
                    scores_T(a, b, 7)
                    for G in range(H // 4):
                        attend(a, b, f, G)

            periods(pe, period)

        @block.scalar
        def _(act):
            def columns_hi(dst, bank):
                return nc.scalar.copy(dst[:], X[:, bank].rearrange("p (k q) -> p k q", k=KD))

            def dense_hi():
                act.wait_ge(wo_w1_loaded, 16 * 2)
                act.wait_ge(dense_small_loaded, DENSE_SMALL_COUNT)
                nc.scalar.copy(wo_hi[:], wqkvo_in[:, 3]).then_inc(dense_hid, 1)
                for k in range(KD):
                    nc.scalar.activation(w1_hi[:, k], w1_in[:, k], ACT.Identity, scale=cols[:, 5, k:k + 1]
                                         ).then_inc(dense_hid, 1)
                act.wait_ge(w2_loaded, 16)
                nc.scalar.activation(w2_hi[:], w2_in, ACT.Identity, scale=0.5).then_inc(dense_hid, 1)

            def period(act, g, f, a, b, d, e):
                def copy_attention(i):
                    act.wait_ge(pv_ps, done(b, 2, i + 1))
                    nc.scalar.copy(aug[:, 2 * i:2 * i + 2], X[:, 2 + i].rearrange("p (g q) -> p g q", g=2)
                                   ).then_inc(aug_set, 1)

                def hidden_hi(u):
                    if d is not None:
                        act.wait_ge(*((act01_set, done(d, 2, u + 1)) if u < 2 else (act23_set, done(d, 2, u - 1))))
                        if u == 0:
                            wait(act, f2_ps, number(d))
                        nc.scalar.copy(a_hi[:, u], act_f[:, u]).then_inc(a_hid, 1)

                def gate(u):
                    if d is not None:
                        act.wait_ge(f1_ps, done(d, NU, u + 1))
                        wait(act, *((act23_set, 2 * number(d) + u - 1) if u < 2 else (act01_set, done(d, 2, u - 1))))
                        halves = [(slice(i * LQ, (i + 1) * LQ), slice(2 * u + i, 2 * u + i + 1)) for i in range(2)]
                        for q, m in halves:
                            nc.scalar.activation(th[:, u % 2, q], X[:, 2 + u % 2, q], ACT.Tanh, bias=b1_half[:, m], scale=0.5)
                        for q, m in halves:
                            last = nc.scalar.activation(hid[:, u % 2, q], X[:, 2 + u % 2, q], ACT.Identity, bias=b1_col[:, m])
                        last.then_inc(hid_set, 1)

                if e is not None:
                    act.wait_ge(x2_mined, done(e))
                    wait(act, q_phi_set, number(e))
                    nc.scalar.activation(x2_exp, x2_min, ACT.Exp).then_inc(x2_exped, 1)
                if b is not None:
                    wait(act, aug_ps, number(b))
                    copy_attention(0)
                    copy_attention(1)
                if f is not None:
                    act.wait_ge(cT_ps, done(f))
                    wait(act, kv_rows_ps, number(f))
                    nc.scalar.copy(cT_hi[:], X[:, 0, 0:KD * LK].rearrange("p (k q) -> p k q", k=KD)).then_inc(cT_hid, 1)
                if e is not None:
                    act.wait_ge(qpT_ps, done(e))
                    wait(act, la_ps, QT * number(e))
                    columns_hi(qpT_hi, 1).then_inc(qpT_hid, 1)
                if f is not None:
                    act.wait_ge(kv_rows_ps, done(f))
                    wait(act, k_ps, number(f))
                    nc.scalar.copy(k_rows[:], X[0:LK, 3, 0:D]).then_inc(k_copied, 1)
                    wait(act, pv_ps, 2 * (number(f) - 1))
                    for g_ in range(KD):
                        last = nc.scalar.copy(
                            v_aug[:, f.slot].rearrange("k (j g a) w -> k g j a w", g=KD, a=2)[:, g_, :, :, 0:DH],
                            X[0:LK, 3, D + g_ * P:D + (g_ + 1) * P].rearrange("k (j a e) -> k j a e", a=2, e=DH))
                    last.then_inc(v_copied, 1)
                if a is not None:
                    act.wait_ge(c_loaded[a.slot], 16 * (a.half + 1))
                    nc.scalar.activation(c_min[:], cs[:, a.slot], ACT.Relu, scale=-1.0).then_inc(c_mined, 1)
                    act.wait_ge(c_mined, done(a))
                    wait(act, k_phi_set, number(a))
                    nc.scalar.activation(c_exp[:], c_min[:], ACT.Exp, scale=-1.0).then_inc(c_exped, 1)
                if b is not None:
                    act.wait_ge(cnT_ps, done(b))
                    wait(act, wo_ps, number(b))
                    columns_hi(cnT_hi, 0).then_inc(cnT_hid, 1)
                gate(0)
                if f is not None:
                    act.wait_ge(k_ps, done(f))
                    wait(act, k_stacked, 16 * K_DMAS * number(f))
                    if is_first(f):
                        act.wait_ge(small_loaded, SMALL_COUNT)
                    for g_ in range(KD):
                        nc.scalar.activation(k_hi[:, g_], X[:, 1, g_ * LK:(g_ + 1) * LK], ACT.Identity,
                                             bias=cols[:, 1, g_:g_ + 1]).then_inc(k_hid, 1)
                gate(1)
                hidden_hi(0)
                gate(2)
                if f is not None:
                    act.wait_ge(xT_ps, done(f))
                    wait(act, q_ps, number(f))
                    columns_hi(xT_hi, 1).then_inc(xT_hid, 1)
                    if is_first(f):
                        dense_hi()
                hidden_hi(1)
                gate(3)
                hidden_hi(2)
                if b is not None:
                    act.wait_ge(hT_ps, done(b))
                    wait(act, f1_ps, NU * number(b))
                    nc.scalar.copy(hT_hi[:], S[:, 1].rearrange("p (k q) -> p k q", k=KD)).then_inc(hT_hid, 1)
                hidden_hi(3)
                if f is not None:
                    act.wait_ge(q_ps, done(f))
                    wait(act, q_stacked, 16 * Q_DMAS * number(f))
                    if is_first(f):
                        act.wait_ge(bq_set, 2)
                    for g_ in range(KD):
                        nc.scalar.activation(q_hi[:, g_], X[:, 1, g_ * LQ:(g_ + 1) * LQ], ACT.Identity,
                                             bias=bq_col[:, g_:g_ + 1]).then_inc(q_hid, 1)
                if b is not None:
                    wait(act, la_ps, QT * (number(b) - 1))
                    for c in range(KD):
                        act.wait_ge(kv_ps, done(b, KD, c + 1))
                        nc.scalar.copy(kv_hi[:, b.slot, c], X[:, 2 + c, 0:KVW]).then_inc(kv_hid, 1)
                if a is not None:
                    if is_first(a):
                        act.wait_ge(rows_ps, 1)
                    wait(act, pv_ps, 2 * number(a))
                    for p in range(PAIRS):
                        act.wait_ge(st_ps, done(a, PAIRS, p + 1))
                        nc.scalar.activation(probs[:, 2 * p:2 * p + 2], S[0:LK, p % 4].rearrange("k (h q) -> k h q", h=2),
                                             ACT.Exp).then_inc(probs_set, 1)

            act.wait_ge(wq_ordered, 1)
            act.wait_ge(gain_set, 1)
            for k in range(KD):
                last = nc.scalar.activation(wq_hi[:, k], wq_raw[:, k], ACT.Identity, scale=q_gain[:, k:k + 1])
            last.then_inc(w_hid, 1)
            act.wait_ge(wkv_loaded, 16 * 2)
            for dst, src in zip(chunks(wkv_hi, permuted), chunks(wqkvo_in[:, 1], raw)):
                last = nc.scalar.copy(dst, src)
            last.then_inc(w_hid, 1)
            nc.scalar.copy(wkv_hi[:, :, D:2 * D], wqkvo_in[:, 2]).then_inc(w_hid, 1)
            act.wait_ge(fixed_set, FIXED_COUNT)

            periods(act, period)

        @block.vector
        def _(dve):
            V = nc.vector
            V.memset(ones[:], 1.0).then_inc(ones_set, 1)
            dve.wait_ge(wq_loaded, 16)
            for dst, src in zip(chunks(wq_raw, permuted), chunks(wqkvo_in[:, 0], raw)):
                last = V.tensor_copy(dst, src)
            last.then_inc(wq_ordered, 1)
            dve.wait_ge(gain_loaded, 16)
            V.tensor_scalar(q_gain[:], cols[:, 3], SCALE, None, ALU.mult).then_inc(gain_set, 1)

            def set_up_projections():
                dve.wait_ge(wkv_loaded, 16 * 2)
                dve.wait_ge(w_hid, 2)
                for dst, src, hi in zip(chunks(wkv_lo, permuted), chunks(wqkvo_in[:, 1], raw), chunks(wkv_hi, permuted)):
                    V.tensor_tensor(dst, src, hi.bitcast(F32), ALU.subtract)
                dve.wait_ge(w_hid, 3)
                V.tensor_tensor(wkv_lo[:, :, D:2 * D], wqkvo_in[:, 2], wkv_hi[:, :, D:2 * D].bitcast(F32),
                                ALU.subtract).then_inc(proj_set, 1)

            def set_up_query():
                dve.wait_ge(small_loaded, SMALL_COUNT)
                dve.wait_ge(gain_set, 1)
                dve.wait_ge(w_hid, 1)
                for k in range(KD):
                    V.scalar_tensor_tensor(out=wq_lo[:, k], in0=wq_raw[:, k], scalar=q_gain[:, k:k + 1],
                                           in1=wq_hi[:, k].bitcast(F32), op0=ALU.mult, op1=ALU.subtract)
                dve.wait_ge(bq_ps, 1)
                V.tensor_tensor(bq_sum[:], S[:, 3, 0:KD], cols[:, 0], ALU.add).then_inc(bq_set, 1)
                dve.wait_ge(bq_set, 1)
                V.tensor_scalar(bq_col[:], bq_sum[:], SCALE, None, ALU.mult).then_inc(bq_set, 1)

            def max_row_ones():
                dve.wait_ge(fixed_set, 1)
                V.memset(k_stack[96:98, 0].bitcast(F32), 1.0).then_inc(k_fixed, 1)
                V.memset(k_stack[96:100, 1].bitcast(F32), 1.0).then_inc(k_fixed, 1)
                dve.wait_ge(k_fixed, 2)
                V.memset(k_stack[96:98, 1].bitcast(F32), 0.0).then_inc(k_fixed, 1)

            def spread_bv():
                dve.wait_ge(dense_small_loaded, DENSE_SMALL_COUNT)
                for k in range(KD):
                    last = V.tensor_scalar(bv_wide[:, k], ones[:, 0:P], cols[:, 2, k:k + 1], None, ALU.mult)
                last.then_inc(bv_spread, 1)

            def dense_lo():
                dve.wait_ge(dense_hid, 1)
                V.tensor_tensor(wo_lo[:], wqkvo_in[:, 3], wo_hi[:].bitcast(F32), ALU.subtract)
                for k in range(KD):
                    dve.wait_ge(dense_hid, 2 + k)
                    V.scalar_tensor_tensor(out=w1_lo[:, k], in0=w1_in[:, k], scalar=cols[:, 5, k:k + 1],
                                           in1=w1_hi[:, k].bitcast(F32), op0=ALU.mult, op1=ALU.subtract)
                dve.wait_ge(dense_hid, 4)
                V.scalar_tensor_tensor(out=w2_lo[:], in0=w2_in, scalar=0.5, in1=w2_hi[:].bitcast(F32), op0=ALU.mult,
                                       op1=ALU.subtract)

            def dense_rows():
                dve.wait_ge(b1_ps, 1)
                V.tensor_tensor(b1_col[:], S[:, 0, 0:FF // P], b1_raw[:], ALU.add).then_inc(b1_set, 1)
                dve.wait_ge(b1_set, 1)
                V.tensor_scalar(b1_half[:], b1_col[:], 0.5, None, ALU.mult)
                dve.wait_ge(rows_ps, 1)
                V.tensor_copy(bo_all[:], S[:, 2, 0:D])
                V.tensor_copy(b2_all[:], S[:, 2, D:2 * D])
                V.tensor_copy(gamma_all[:], S[:, 3, 0:D])
                V.tensor_copy(beta_all[:], S[:, 3, D:2 * D]).then_inc(dense_set, 1)

            def row_stats(i, src, stat_sem):
                for t in range(QT):
                    last = V.bn_stats(stats[:, i, t], src[:, t])
                last.then_inc(stat_sem, 1)

            def mean_variance(i, stat_sem, mv_sem, b):
                dve.wait_ge(stat_sem, done(b))
                settled(dve)
                for t in range(QT):
                    last = V.bn_aggr(mv[:, i, t], stats[:, i, t])
                last.then_inc(mv_sem, 1)

            def norm_apply(i, dst, src):
                for t in range(QT):
                    last = V.tensor_scalar(dst[:, t], src[:, t], mv[:, i, t, 0:1], rstd[:, i, t:t + 1],
                                           ALU.subtract, ALU.mult)
                return last

            def lo_part(dst, src, hi):
                return V.tensor_tensor(dst, src, hi.bitcast(F32), ALU.subtract)

            def bank(b):
                return X[:, b].rearrange("p (k q) -> p k q", k=KD)

            def flat(tile):
                return tile.rearrange("p t e -> p (t e)")

            def maxima(a, t, half):
                dve.wait_ge(s_ps, done(a, 2 * QT, 2 * t + half + 1))
                banks = slice(2 * half, 2 * half + 2)
                V.tensor_reduce(neg_max[:, t].rearrange("p (b h) -> p b h", b=4)[:, banks],
                                S[:, banks, 0:4 * LK].rearrange("p b (h k) -> p b h k", h=4),
                                axis=AX.X, op=ALU.max, negate=True).then_inc(max_set, 1)

            def hidden(d, u):
                dve.wait_ge(hid_set, done(d, NU, u + 1))
                wait(dve, a_split, NU * number(d))
                V.scalar_tensor_tensor(out=act_f[:, u], in0=th[:, u % 2], scalar=1.0, in1=hid[:, u % 2],
                                       op0=ALU.add, op1=ALU.mult).then_inc(act23_set, 1)

            def residual_out(e):
                dve.wait_ge(la_ps, done(e, QT))
                V.tensor_scalar(z_den[:], S[:, 2:4, D], Z_EPS, None, ALU.add).then_inc(z_set, 1)
                dve.wait_ge(z_set, done(e))
                V.reciprocal(z_inv[:], z_den[:]).then_inc(z_inved, 1)
                dve.wait_ge(z_inved, done(e))
                wait(dve, y_set, number(e))
                for t in range(QT):
                    last = V.scalar_tensor_tensor(out=x3[:, t], in0=S[:, 2 + t, 0:D], scalar=z_inv[:, t:t + 1],
                                                  in1=x2[:, t], op0=ALU.mult, op1=ALU.add)
                last.then_inc(x3_set, 1)

            def attention_out(d):
                dve.wait_ge(aug_ps, done(d))
                heads = S[:, 0:QT].rearrange("p t (h w) -> p t h w", w=VW)
                V.reciprocal(den_inv[:], heads[:, :, :, DH]).then_inc(den_set, 1)
                dve.wait_ge(den_set, done(d))
                wait(dve, cnT_ps, number(d))
                for t in range(QT):
                    for g in range(KD):
                        val = heads[:, t, :, 0:DH].rearrange("p (j g a) e -> p g j a e", g=KD, a=2)[:, g]
                        inv = den_inv[:, t].rearrange("p (j g a) -> p g j a", g=KD, a=2)[:, g]
                        last = V.tensor_tensor(cn[:, t, g * P:(g + 1) * P].rearrange("p (j a e) -> p j a e", a=2, e=DH),
                                               val, inv[:, :, :, None].to_broadcast([P, H // 4, 2, DH]), ALU.mult)
                last.then_inc(cn_set, 1)

            def normalise_x(f):
                dve.wait_ge(rstd1, done(f))
                wait(dve, xT_ps, number(f))
                norm_apply(0, xn, xs[:, f.slot]).then_inc(xn_set, 1)

            def elu_x2(e, f):
                dve.wait_ge(f2_ps, done(e))
                dve.wait_ge(x1_b2_set, done(e))
                V.tensor_tensor(x2, bank(0), x1_b2[:, e.slot], ALU.add).then_inc(x2_set, 1)
                dve.wait_ge(x2_set, done(e))
                wait(dve, x2_exped, number(e))
                V.tensor_scalar(x2_min, x2, 0.0, None, ALU.min).then_inc(x2_mined, 1)
                if f is not None:
                    normalise_x(f)
                dve.wait_ge(x2_exped, done(e))
                wait(dve, qpT_ps, number(e))
                V.scalar_tensor_tensor(out=flat(q_phi), in0=flat(x2_exp), scalar=-1.0, in1=flat(x2), op0=ALU.add,
                                       op1=ALU.max).then_inc(q_phi_set, 1)

            def period(dve, g, f, a, b, d, e):
                if e is not None:
                    elu_x2(e, f)
                elif f is not None:
                    normalise_x(f)
                if f is not None:
                    dve.wait_ge(cT_hid, done(f))
                    lo_part(cT_lo[:], X[:, 0, 0:KD * LK].rearrange("p (k q) -> p k q", k=KD), cT_hi[:]).then_inc(cT_split, 1)
                    if is_first(f):
                        max_row_ones()
                    if a is not None and is_first(a):
                        dense_rows()
                if e is not None:
                    dve.wait_ge(qpT_hid, done(e))
                    lo_part(qpT_lo[:], bank(1), qpT_hi[:]).then_inc(qpT_split, 1)
                if b is not None:
                    attention_out(b)
                if e is not None:
                    residual_out(e)
                if b is not None:
                    dve.wait_ge(cnT_hid, done(b))
                    lo_part(cnT_lo[:], bank(0), cnT_hi[:]).then_inc(cnT_split, 1)
                if a is not None:
                    maxima(a, 0, 0)
                    maxima(a, 0, 1)
                if f is not None:
                    dve.wait_ge(k_hid, done(f, KD))
                    if is_first(f):
                        dve.wait_ge(small_loaded, SMALL_COUNT)
                    for c in range(KD):
                        last = V.scalar_tensor_tensor(out=k_lo[:, c], in0=X[:, 1, c * LK:(c + 1) * LK],
                                                      scalar=cols[:, 1, c:c + 1], in1=k_hi[:, c].bitcast(F32), op0=ALU.add,
                                                      op1=ALU.subtract)
                    last.then_inc(k_split, 1)
                    if is_first(f):
                        set_up_query()
                if b is not None:
                    dve.wait_ge(wo_ps, done(b))
                    dve.wait_ge(x_bo_set, done(b))
                    wait(dve, x1_b2_set, number(b))
                    V.tensor_tensor(x1[:], bank(0), x_bo[:], ALU.add).then_inc(x1_set, 1)
                    dve.wait_ge(x1_set, done(b))
                    row_stats(1, x1, stat2)
                if b is not None:
                    mean_variance(1, stat2, mv2, b)
                if a is not None:
                    maxima(a, 1, 0)
                if a is not None:
                    maxima(a, 1, 1)
                if a is not None:
                    dve.wait_ge(max_set, done(a, 2 * QT))
                    wait(dve, maxT_ps, number(a))
                    part = max_parts[:].rearrange("p t (a l m) -> p l t m a", a=2, l=2)
                    neg = neg_max[:].rearrange("p t (m a) -> p t m a", a=2)
                    for t in range(QT):
                        last = V.tensor_copy(part[:, 0, t], neg[:, t])
                    last.then_inc(max_hid, 1)
                    dve.wait_ge(max_hid, done(a))
                    for t in range(QT):
                        last = lo_part(part[:, 1, t], neg[:, t], part[:, 0, t])
                    last.then_inc(max_split, 1)
                if f is not None:
                    dve.wait_ge(xT_hid, done(f))
                    lo_part(xT_lo[:], bank(1), xT_hi[:]).then_inc(xT_split, 1)
                    if is_first(f):
                        spread_bv()
                        dense_lo()
                if b is not None:
                    dve.wait_ge(rstd2, done(b))
                    wait(dve, hT_ps, number(b))
                    norm_apply(1, hn, x1).then_inc(hn_set, 1)
                if a is not None:
                    dve.wait_ge(maxT_ps, done(a))
                    wait(dve, max_stacked, 16 * number(a))
                    V.tensor_copy(max_T[:], S[0:4 * PAIRS, 0, 0:LQ]).then_inc(maxT_set, 1)
                if d is not None:
                    hidden(d, 2)
                    hidden(d, 3)
                if b is not None:
                    dve.wait_ge(hT_hid, done(b))
                    lo_part(hT_lo[:], S[:, 1].rearrange("p (k q) -> p k q", k=KD), hT_hi[:]).then_inc(hT_split, 1)
                if e is not None:
                    dve.wait_ge(x3_set, done(e))
                    wait(dve, rstd3, number(e))
                    row_stats(2, x3, stat3)
                if a is not None:
                    dve.wait_ge(c_exped, done(a))
                    wait(dve, kp_split, number(a))
                    V.scalar_tensor_tensor(out=k_phi[:], in0=c_exp[:], scalar=-1.0, in1=cs[:, a.slot], op0=ALU.add,
                                           op1=ALU.max).then_inc(k_phi_set, 1)
                if f is not None:
                    dve.wait_ge(q_hid, done(f, KD))
                    for c in range(KD):
                        last = V.scalar_tensor_tensor(out=q_lo[:, c], in0=X[:, 1, c * LQ:(c + 1) * LQ],
                                                      scalar=bq_col[:, c:c + 1], in1=q_hi[:, c].bitcast(F32), op0=ALU.add,
                                                      op1=ALU.subtract)
                    last.then_inc(q_split, 1)
                if b is not None:
                    dve.wait_ge(kv_hid, done(b, KD))
                    for c in range(KD):
                        lo_part(kv_lo[:, b.slot, c], X[:, 2 + c, 0:KVW], kv_hi[:, b.slot, c]).then_inc(kv_split, 1)
                if a is not None:
                    dve.wait_ge(k_phi_set, done(a))
                    wait(dve, kv_ps, KD * number(a))
                    V.tensor_copy(kp_hi[:], k_phi[:]).then_inc(kp_hid, 1)
                if e is not None:
                    mean_variance(2, stat3, mv3, e)
                if g is not None:
                    dve.wait_ge(x_loaded[g.slot], 16 * (g.half + 1))
                    wait(dve, rstd1, number(g))
                    row_stats(0, xs[:, g.slot], stat1)
                if a is not None:
                    dve.wait_ge(kp_hid, done(a))
                    lo_part(kp_lo[:], k_phi[:], kp_hi[:]).then_inc(kp_split, 1)
                if g is not None:
                    mean_variance(0, stat1, mv1, g)

            periods(dve, period, set_up_projections)

        @block.gpsimd
        def _(pool):
            G = nc.gpsimd
            G.memset(ident[:], 0.0).then_inc(ident_set, 1)
            pool.wait_ge(ident_set, 1)
            G.affine_select(out=ident[:], in_=ident[:], compare_op=ALU.not_equal, fill=1.0, base=0,
                            pattern=[[-1, P]], channel_multiplier=1).then_inc(ident_set, 1)
            G.memset(minus_half[:], -0.5)
            G.memset(k_stack[:].bitcast(F32), 0.0).then_inc(fixed_set, 1)
            G.memset(v_aug[:], 0.0).then_inc(fixed_set, 1)
            pool.wait_ge(fixed_set, 2)
            G.memset(v_aug[:, :, :, DH:DH + 1], 1.0).then_inc(fixed_set, 1)
            G.memset(c_hi[:, D:D + 1].bitcast(F32), 1.0)
            G.memset(c_hi[:, D + 1:KVW].bitcast(F32), 0.0)
            G.memset(c_lo[:, D:KVW].bitcast(F32), 0.0).then_inc(fixed_set, 1)

            def inverse_deviation(i, mv_sem, var_sem, rstd_sem, b):
                pool.wait_ge(mv_sem, done(b))
                settled(pool)
                G.tensor_scalar(var_eps[:, i], mv[:, i, :, 1], 1.0, LN_EPS, ALU.mult, ALU.add).then_inc(var_sem, 1)
                pool.wait_ge(var_sem, done(b))
                G.tensor_tensor(rstd[:, i], var_eps[:, i], minus_half[:], ALU.pow).then_inc(rstd_sem, 1)

            def finish(d):
                inverse_deviation(2, mv3, var3, rstd3, d)
                pool.wait_ge(rstd3, done(d))
                G.tensor_tensor(mean_rstd[:], mv[:, 2, :, 0], rstd[:, 2], ALU.mult).then_inc(mean_set, 1)
                pool.wait_ge(mean_set, done(d))
                settled(pool)
                G.tensor_scalar(mean_shift[:], mean_rstd[:], -1.0, 0.0, ALU.mult, ALU.add).then_inc(shift_set, 1)
                pool.wait_ge(shift_set, done(d))
                settled(pool)
                for t in range(QT):
                    last = G.tensor_scalar(y[:, t], x3[:, t], rstd[:, 2, t:t + 1], mean_shift[:, t:t + 1],
                                           ALU.mult, ALU.add)
                last.then_inc(y_set, 1)
                pool.wait_ge(y_set, done(d))
                for t in range(QT):
                    last = G.tensor_tensor(yg[:, t], y[:, t], gamma_all[:], ALU.mult)
                last.then_inc(yg_set, 1)
                pool.wait_ge(yg_set, done(d))
                wait(pool, stored, 16 * number(d))
                for t in range(QT):
                    last = G.tensor_tensor(y_out[:, t], yg[:, t], beta_all[:], ALU.add)
                last.then_inc(y_out_set, 1)

            def period(pool, g, f, a, b, d, e):
                def hidden_lo(u):
                    if d is not None:
                        pool.wait_ge(a_hid, done(d, NU, u + 1))
                        if u == 0:
                            wait(pool, f2_ps, number(d))
                        G.tensor_tensor(a_lo[:, u], act_f[:, u], a_hi[:, u].bitcast(F32), ALU.subtract).then_inc(a_split, 1)

                def hidden(u):
                    if d is not None:
                        pool.wait_ge(hid_set, done(d, NU, u + 1))
                        settled(pool)
                        G.tensor_scalar(th[:, u], th[:, u], 1.0, 1.0, ALU.mult, ALU.add).then_inc(plus_set, 1)
                        pool.wait_ge(plus_set, done(d, 2, u + 1))
                        wait(pool, a_split, NU * number(d))
                        G.tensor_tensor(act_f[:, u], th[:, u], hid[:, u], ALU.mult).then_inc(act01_set, 1)

                hidden(0)
                hidden_lo(0)
                if b is not None:
                    inverse_deviation(1, mv2, var2, rstd2, b)
                hidden(1)
                hidden_lo(1)
                if a is not None:
                    if is_first(a):
                        pool.wait_ge(dense_set, 1)
                    pool.wait_ge(x_loaded[a.slot], 16 * (a.half + 1))
                    wait(pool, x1_set, number(a))
                    for t in range(QT):
                        last = G.tensor_tensor(x_bo[:, t], xs[:, a.slot, t], bo_all[:], ALU.add)
                    last.then_inc(x_bo_set, 1)
                hidden_lo(2)
                hidden_lo(3)
                if a is not None:
                    pool.wait_ge(c_loaded[a.slot], 16 * (a.half + 1))
                    wait(pool, kv_ps, KD * number(a))
                    settled(pool)
                    G.tensor_scalar(c_hi[:, 0:D], cs[:, a.slot], 1.0, 0.0, ALU.mult, ALU.add).then_inc(c_hid, 1)
                    pool.wait_ge(c_hid, done(a))
                    G.tensor_tensor(c_lo[:, 0:D], cs[:, a.slot], c_hi[:, 0:D].bitcast(F32), ALU.subtract).then_inc(c_split, 1)
                if b is not None:
                    pool.wait_ge(x1_set, done(b))
                    wait(pool, x2_set, number(b) - 1)
                    for t in range(QT):
                        last = G.tensor_tensor(x1_b2[:, b.slot, t], x1[:, t], b2_all[:], ALU.add)
                    last.then_inc(x1_b2_set, 1)
                if g is not None:
                    inverse_deviation(0, mv1, var1, rstd1, g)
                if e is not None:
                    finish(e)

            periods(pool, period)


_INS = ['x', 'ctx_1024', 'L0_xattn_Wq', 'L0_xattn_bq', 'L0_xattn_Wk', 'L0_xattn_bk', 'L0_xattn_Wv', 'L0_xattn_bv',
        'L0_xattn_Wo', 'L0_xattn_bo', 'L0_xattn_W1', 'L0_xattn_b1', 'L0_xattn_W2', 'L0_xattn_b2', 'L0_xattn_ln_q_g',
        'L0_xattn_ln_q_b', 'L0_xattn_ln_ff_g', 'L0_xattn_ln_ff_b', 'L1_xattn_gamma', 'L1_xattn_beta']


def kernel(**inputs):
    import numpy as _np
    import concourse.bacc as _bacc
    from concourse import mybir as _mybir
    from concourse.bass_utils import run_bass_kernel_spmd as _run

    nc = _bacc.Bacc("TRN2", target_bir_lowering=False, num_devices=1)
    arrays, args = {}, []
    for name in _INS:
        a = _np.ascontiguousarray(inputs[name])
        arrays[f"in_{name}_dram"] = a
        args.append(nc.dram_tensor(f"in_{name}_dram", a.shape, _mybir.dt.from_np(a.dtype), kind="ExternalInput").ap())
    args.append(nc.dram_tensor("out_0_dram", inputs["x"].shape, _mybir.dt.float32, kind="ExternalOutput").ap())
    build(nc, *args)
    r = _run(nc, [arrays], core_ids=[0])
    return r.results[0]["out_0_dram"]
```
